# Optimizing a Trainium2 kernel written in Bass

```python
import numpy as np
import jax
import jax.numpy as jnp

def _softmax(x, axis=-1):
    return jax.nn.softmax(x, axis=axis)

def _gelu(x):
    return jax.nn.gelu(x, approximate=True)

def _silu(x):
    return jax.nn.silu(x)

def _sigmoid(x):
    return jax.nn.sigmoid(x)

def _layernorm(x, axis=-1, eps=1e-05):
    m = jnp.mean(x, axis=axis, keepdims=True)
    v = jnp.var(x, axis=axis, keepdims=True)
    return (x - m) / jnp.sqrt(v + eps)

def _scatter_add(tgt, idx, src, axis=0):
    return tgt.at[idx].add(src)

def _segment_sum(src, seg, n):
    return jax.ops.segment_sum(src, seg, n)
kernel_name = 'mk_adaln_attn_ffn_d1_seqx_r8_145756'

def setup_inputs(seed: int=0):
    np.random.seed(seed)
    _w = jnp.asarray

    def _rec_inputs():
        import jax
        import jax.numpy as jnp
        _rk = jax.random.key(seed)
        x = -7.109e-05 + 0.9999 * jax.random.normal(jax.random.fold_in(_rk, 1), (128, 32, 512), jnp.float32)
        _lenS = 32 - jax.random.randint(jax.random.fold_in(_rk, 7), (128,), 0, max(1, 32 // 4) + 1, jnp.int32)
        _lenS2 = 32 - jax.random.randint(jax.random.fold_in(_rk, 8), (128,), 0, max(1, 32 // 4) + 1, jnp.int32)
        itok_B_0_15 = jax.random.randint(jax.random.fold_in(_rk, 11), (128,), 0, 16, jnp.int32)
        itok_B_0_2 = jax.random.randint(jax.random.fold_in(_rk, 12), (128,), 0, 3, jnp.int32)
        return (x, itok_B_0_15, itok_B_0_2)
    x, itok_B_0_15, itok_B_0_2 = _rec_inputs()

    def _L0_cond_setup():
        import jax, jax.numpy as jnp
        import numpy as np
        NUM_CONDITIONS = 16
        IN_CH = 32
        OUT_CH = 32
        B = 64
        T = 512
        key = jax.random.key(seed)
        k_x, k_w, k_c = jax.random.split(key, 3)
        x = jax.random.normal(k_x, (B, IN_CH, T), dtype=jnp.float32)
        bound = float(np.sqrt(6.0 / IN_CH))
        weights = jax.random.uniform(k_w, (NUM_CONDITIONS, IN_CH, OUT_CH), dtype=jnp.float32, minval=-bound, maxval=bound)
        condition = jax.random.randint(k_c, (B,), 0, NUM_CONDITIONS, dtype=jnp.int64)
        return {'x': x, 'weights': weights, 'condition': condition}
    _L0_cond_all = _L0_cond_setup()
    _L0_cond_in = {k: v for k, v in _L0_cond_all.items() if k in ('weights',)}
    del _L0_cond_all

    def _L0_attn_setup():
        import jax, jax.numpy as jnp
        import numpy as np
        B, S, EMB = (2, 256, 512)
        NHEADS, KVHEADS, HEAD_D = (32, 8, 128)
        SPLITS = (NHEADS * HEAD_D, KVHEADS * HEAD_D, KVHEADS * HEAD_D)
        key = jax.random.key(seed)
        k1, k2, k3 = jax.random.split(key, 3)
        q = jax.random.normal(k1, (B, S, EMB), dtype=jnp.float32)
        w_qkv = jax.random.normal(k2, (sum(SPLITS), EMB), dtype=jnp.float32) * 0.02
        w_dense = jax.random.normal(k3, (EMB, NHEADS * HEAD_D), dtype=jnp.float32) * 0.02
        return {'q': q, 'w_qkv': w_qkv, 'w_dense': w_dense}
    _L0_attn_all = _L0_attn_setup()
    _L0_attn_in = {k: v for k, v in _L0_attn_all.items() if k in ('w_qkv', 'w_dense')}
    del _L0_attn_all

    def _L0_cond2_setup():
        import jax, jax.numpy as jnp
        import numpy as np
        B, S, D_IN, D_OUT = (4, 256, 512, 512)
        R, NUM_LABELERS = (32, 5)
        LORA_SCALING = 16 / 32
        key = jax.random.key(seed)
        k1, k2, k3, k4, k5 = jax.random.split(key, 5)
        x = jax.random.normal(k1, (B, S, D_IN), dtype=jnp.float32)
        labeler_index = jax.random.randint(k2, (B,), 0, NUM_LABELERS, dtype=jnp.int64)
        W = jax.random.normal(k3, (D_OUT, D_IN), dtype=jnp.float32) * 0.02
        lora_A = jax.random.normal(k4, (NUM_LABELERS, D_IN, R), dtype=jnp.float32) * 0.02
        lora_B_w = jax.random.normal(k5, (D_OUT, R), dtype=jnp.float32) * 0.02
        return {'x': x, 'labeler_index': labeler_index, 'W': W, 'lora_A': lora_A, 'lora_B_w': lora_B_w}
    _L0_cond2_all = _L0_cond2_setup()
    _L0_cond2_in = {k: v for k, v in _L0_cond2_all.items() if k in ('W', 'lora_A', 'lora_B_w')}
    del _L0_cond2_all

    def _L0_ffn_setup():
        import jax, jax.numpy as jnp
        import numpy as np
        OUT, IN = (512, 512)
        B, S = (4, 256)

        def _quantize(w):
            min_val, max_val = (jnp.min(w), jnp.max(w))
            scale = (max_val - min_val) / 255.0
            zp = 255.0 - max_val / scale
            zp = jnp.clip(zp, 0.0, 255.0)
            zp = jnp.round(zp)
            q = jnp.round(jnp.clip(zp + w / scale, 0.0, 255.0)).astype(jnp.int32)
            return (q, scale, zp)
        key = jax.random.key(seed)
        kx, kw, kb = jax.random.split(key, 3)
        x = jax.random.normal(kx, (B, S, IN), dtype=jnp.float32)
        w_fp = jax.random.normal(kw, (OUT, IN), dtype=jnp.float32) * 0.02
        bias = jax.random.normal(kb, (OUT,), dtype=jnp.float32) * 0.01
        qweight, scale, zero_point = _quantize(w_fp)
        return {'x': x, 'qweight': qweight, 'scale': scale, 'zero_point': zero_point, 'bias': bias}
    _L0_ffn_all = _L0_ffn_setup()
    _L0_ffn_in = {k: v for k, v in _L0_ffn_all.items() if k in ('qweight', 'scale', 'zero_point', 'bias')}
    del _L0_ffn_all
    return {'x': x, 'itok_B_0_15': itok_B_0_15, 'itok_B_0_2': itok_B_0_2, 'L0_cond_weights': _L0_cond_in['weights'], 'L0_attn_w_qkv': _L0_attn_in['w_qkv'], 'L0_attn_w_dense': _L0_attn_in['w_dense'], 'L0_cond2_W': _L0_cond2_in['W'], 'L0_cond2_lora_A': _L0_cond2_in['lora_A'], 'L0_cond2_lora_B_w': _L0_cond2_in['lora_B_w'], 'L0_ffn_qweight': _L0_ffn_in['qweight'], 'L0_ffn_scale': _L0_ffn_in['scale'], 'L0_ffn_zero_point': _L0_ffn_in['zero_point'], 'L0_ffn_bias': _L0_ffn_in['bias']}

def reference(x, itok_B_0_15, itok_B_0_2, L0_cond_weights, L0_attn_w_qkv, L0_attn_w_dense, L0_cond2_W, L0_cond2_lora_A, L0_cond2_lora_B_w, L0_ffn_qweight, L0_ffn_scale, L0_ffn_zero_point, L0_ffn_bias):
    import jax
    import jax.numpy as jnp

    def _L0_cond_ref(x, weights, condition):
        import jax, jax.numpy as jnp
        import numpy as np
        NUM_CONDITIONS = 16
        IN_CH = 32
        OUT_CH = 32
        B = 64
        T = 512
        W = weights[condition]
        return jnp.einsum('bct,bcd->bdt', x, W)

    def _L0_attn_ref(q, w_qkv, w_dense):
        import jax, jax.numpy as jnp
        import numpy as np
        B, S, EMB = (2, 256, 512)
        NHEADS, KVHEADS, HEAD_D = (32, 8, 128)
        SPLITS = (NHEADS * HEAD_D, KVHEADS * HEAD_D, KVHEADS * HEAD_D)
        Bq, Sq, _ = q.shape
        qkv = q @ w_qkv.T
        qs, ks, vs = jnp.split(qkv, np.cumsum(SPLITS)[:-1], axis=-1)
        G = NHEADS // KVHEADS
        qh = qs.reshape(Bq, Sq, KVHEADS, G, HEAD_D)
        kh = ks.reshape(Bq, Sq, KVHEADS, HEAD_D)
        vh = vs.reshape(Bq, Sq, KVHEADS, HEAD_D)
        scale = 1.0 / jnp.sqrt(jnp.float32(HEAD_D))
        scores = jnp.einsum('bskgd,btkd->bkgst', qh, kh) * scale
        causal = jnp.tril(jnp.ones((Sq, Sq), dtype=bool))
        scores = jnp.where(causal, scores, jnp.finfo(scores.dtype).min)
        probs = jax.nn.softmax(scores, axis=-1)
        attn = jnp.einsum('bkgst,btkd->bskgd', probs, vh)
        attn = attn.reshape(Bq, Sq, NHEADS * HEAD_D)
        return attn @ w_dense.T

    def _L0_cond2_ref(x, labeler_index, W, lora_A, lora_B_w):
        import jax, jax.numpy as jnp
        import numpy as np
        B, S, D_IN, D_OUT = (4, 256, 512, 512)
        R, NUM_LABELERS = (32, 5)
        LORA_SCALING = 16 / 32
        base = jnp.einsum('bsi,oi->bso', x, W)
        labelers_A = lora_A[labeler_index]
        low = jnp.einsum('bsi,bir->bsr', x, labelers_A)
        delta = jnp.einsum('bsr,or->bso', low, lora_B_w) * LORA_SCALING
        return base + delta

    def _L0_ffn_ref(x, qweight, scale, zero_point, bias):
        import jax, jax.numpy as jnp
        import numpy as np
        OUT, IN = (512, 512)
        B, S = (4, 256)

        def _quantize(w):
            min_val, max_val = (jnp.min(w), jnp.max(w))
            scale = (max_val - min_val) / 255.0
            zp = 255.0 - max_val / scale
            zp = jnp.clip(zp, 0.0, 255.0)
            zp = jnp.round(zp)
            q = jnp.round(jnp.clip(zp + w / scale, 0.0, 255.0)).astype(jnp.int32)
            return (q, scale, zp)
        w = scale * (qweight.astype(x.dtype) - zero_point)
        return jnp.einsum('bsi,oi->bso', x, w) + bias
    x = x + _L0_attn_ref(_L0_cond_ref(x, L0_cond_weights, itok_B_0_15), L0_attn_w_qkv, L0_attn_w_dense)
    x = x + _L0_ffn_ref(_L0_cond2_ref(x, itok_B_0_2, L0_cond2_W, L0_cond2_lora_A, L0_cond2_lora_B_w), L0_ffn_qweight, L0_ffn_scale, L0_ffn_zero_point, L0_ffn_bias)
    return x

_drawn_inputs = setup_inputs


def setup_inputs(seed=0):
    import zlib

    import numpy as np

    out = dict(_drawn_inputs(seed))
    spreads = {}
    factors = {'L0_cond2_lora_A': 5.009, 'L0_cond2_lora_B_w': 4.958, 'L0_ffn_bias': 6.082}
    for name, (base, spread) in spreads.items():
        noise = np.random.default_rng([zlib.crc32(name.encode()), seed]).standard_normal(out[name].shape)
        drawn = base * np.exp(spread * noise) if base else spread * noise
        out[name] = jnp.asarray(drawn.astype(out[name].dtype))
    for name, factor in factors.items():
        out[name] = (out[name] * factor).astype(out[name].dtype)
    return out
```

```python
from contextlib import ExitStack

import concourse.bass as bass
from concourse import mybir
from concourse.alu_op_type import AluOpType as ALU


def adaln_attention_ffn_kernel(
    nc: bass.Bass,
    x: bass.AP,
    cond_index: bass.AP,
    label_index: bass.AP,
    w_cond: bass.AP,
    w_qkv: bass.AP,
    w_dense: bass.AP,
    w_base: bass.AP,
    lora_a: bass.AP,
    lora_b: bass.AP,
    q_ffn: bass.AP,
    ffn_scale: bass.AP,
    ffn_zero: bass.AP,
    ffn_bias: bass.AP,
    out: bass.AP,
):
    f32, f16, i32 = mybir.dt.float32, mybir.dt.float16, mybir.dt.int32
    ACT = mybir.ActivationFunctionType
    AX = mybir.AxisListType
    RED = bass.bass_isa.ReduceOp

    P = 128
    B, S, E = x.shape
    NCOND = w_cond.shape[0]
    NLAB, _, R = lora_a.shape
    HEADS, KV, D = 32, 8, 128
    G = HEADS // KV
    NC = E // P
    TOK = B * S
    TILES = TOK // P
    TB = P // S
    BB = 8
    BT = BB * S
    BTILES = BT // P
    BLOCKS = B // BB
    WT = G + 2 + NC
    KT, VT, DT = G, G + 1, G + 2
    PREP_AT = BLOCKS - WT
    VDMAS = TB * 4

    IDENTS_TURN, POOL_TURNS = 4, 13
    SPLIT = 2.0 ** 15
    EVAC = 2.0 ** -24
    MASKED = -3.0e38

    x_t = x.rearrange("(n a) s e -> (a s) n e", a=TB)
    out_t = out.rearrange("(n a) s e -> n (a s) e", a=TB)
    gathered = nc.dram_tensor("gathered", [B, S * S], f32, kind="Internal").ap()

    ctx = ExitStack()
    with ctx:
        def sb(name, shape, dt=f32):
            return ctx.enter_context(nc.sbuf_tensor(name, shape, dt))

        def pb(name, shape, dt=f32):
            return ctx.enter_context(nc.psum_tensor(name, shape, dt))

        def sem(name):
            return ctx.enter_context(nc.semaphore(name))

        X2 = sb("X2", [P, TILES, E])
        CH = sb("CH", [P, NC, TOK], f16)
        CL = sb("CL", [P, NC, TOK], f16)
        WN = [sb(f"WN{p}", [P, WT, E]) for p in range(2)]
        WH = [w[:, :, :].bitcast(f16).rearrange("p r (h c d) -> p r h c d", h=2, c=NC) for w in WN]
        ST = sb("ST", [P, E])
        QH = sb("QH", [P, BB, G, S], f16)
        QL = sb("QL", [P, BB, G, S], f16)
        KHL = sb("KHL", [P, BB, 2, S], f16)
        VHL = sb("VHL", [P, BTILES, 2, D], f16)
        VST = sb("VST", [P, BB, D], f16)
        PST = sb("PST", [P, BB, 4, S], f16)
        PT = sb("PT", [P, BB, P], f16)
        AH = sb("AH", [P, G, BT], f16)
        AL = sb("AL", [P, G, BT], f16)
        S1 = sb("S1", [P, BB, S])
        S2 = sb("S2", [P, BB, S])
        PR = sb("PR", [P, BB, S])
        mask = sb("mask", [P, S])
        ident = sb("ident", [P, P])
        ident16 = sb("ident16", [P, P], f16)
        smax = sb("smax", [P, BB])
        ssum = sb("ssum", [P, BB])
        srec = sb("srec", [P, BB])
        M = sb("M", [P, NC, E])
        LA = sb("LA", [P, NC, NLAB, R])
        LB = sb("LB", [R + 1, E])
        onehot = sb("onehot", [P, TILES, NLAB])
        wts = [sb(f"wts{p}", [P, WT]) for p in range(2)]
        label = sb("label", [P, TILES, TB], i32)
        cidx = sb("cidx", [P, 1], i32)
        xmaxs = sb("xmaxs", [P, 10])
        wmaxs = sb("wmaxs", [P, WT // 2])
        bounds = sb("bounds", [P, 8])
        wsc = [sb(f"wsc{p}", [P, 12]) for p in range(2)]
        fsc = sb("fsc", [P, 2])

        chf = CH[:, :, :].rearrange("p c t -> p (c t)").bitcast(f32)
        wbase_n = chf[:, 0:NC * E].rearrange("p (c e) -> p c e", c=NC)
        wffn_f = chf[:, NC * E:2 * NC * E].rearrange("p (c e) -> p c e", c=NC)
        wffn_t = chf[:, 2 * NC * E:3 * NC * E].rearrange("p (c e) -> p c e", c=NC)
        wffn_q = chf[:, 3 * NC * E:4 * NC * E].bitcast(i32).rearrange("p (c e) -> p c e", c=NC)
        clf = CL[:, :, :].rearrange("p c t -> p (c t)").bitcast(f32)
        lorab_n = clf[:, 0:NC * R].rearrange("p (c r) -> p c r", c=NC)
        wcond_n = clf[:, 256:384]
        gath = clf[:, 1024:1024 + S * S]
        wn1 = WN[1][:, :, :].rearrange("p r e -> p (r e)")
        bd = wn1[:, 0:TILES * P].rearrange("p (n t) -> p n t", n=TILES)
        wn0 = WN[0][:, :, :].rearrange("p r e -> p (r e)")
        XS = [wn0[:, n * E:(n + 1) * E] for n in range(2)]
        XT = [wn0[:, (2 + n) * E:(3 + n) * E].rearrange("p (c t) -> p c t", c=NC) for n in range(2)]
        OT = [wn0[:, (4 + n) * E:(5 + n) * E] for n in range(2)]
        LOWM = wn0[:, 6 * E:6 * E + NLAB * R].rearrange("p (l r) -> p l r", l=NLAB)
        LOW = [wn0[:, 7 * E + 256 * n:7 * E + 256 * n + R] for n in range(2)]
        LOWT = [wn0[0:R + 1, 8 * E + 256 * n:8 * E + 256 * n + P] for n in range(2)]

        pQ = [pb(f"pQ{n}", [P, 512]) for n in range(2)]
        pKV = pb("pKV", [P, 512])
        pS = pb("pS", [P, 512])
        pT = pb("pT", [P, 512])
        pA = [pb(f"pA{n}", [P, 512]) for n in range(2)]
        pD = pb("pD", [P, 512])
        pT16 = pT[:, :].bitcast(f16)

        names = """ffnw_in x_in small_in cond_in gath_in gath_out bd_in wn_in v_stacked out_done
            pool_turn dense_zeroed chain ffn_ready ffn_t ffn_tc m_done m_copied
            xmax_ready bounds_ready cscale_ready c_done c_hi c_lo onehot_ready
            stage_full w_t w_hi w_lo wscale_ready escale_ready wmax_part wmax_ready wmax_all xmax_all
            k_done q_done v_done s_done t_done a_done d_done
            k_hi k_lo q_hi q_lo v_hi v_lo pt_copied a_hi a_lo s_read s_sub exp_done p_full p_hi p_lo x2_done
            xs_ready xt_t xt_copied y_done low_done low_sel low_t lowt_copied yb_done ot_ready one_ready""".split()
        s = {n: sem(n) for n in names}
        FREE, FREE_DMA = 1, 16

        def half_of(par, r, h):
            if isinstance(r, int):
                return WH[par][:, r, h, :, :]
            return WH[par][:, bass.ds(r, 1), h, :, :].rearrange("p o c d -> p (o c) d")

        def two_heads(q, n):
            return q[:, :, 2 * n:2 * n + 2, :].rearrange("p b g t -> p b (g t)")

        def chunks(ap):
            return ap.rearrange("p (c d) -> p c d", c=NC)

        block = ctx.enter_context(nc.Block())

        def steps(eng, first, rest):
            with eng.Fori(0, KV // 2) as pair:
                for par in range(2):
                    base = pair * (2 * BLOCKS) + par * BLOCKS
                    first(base, par, pair)
                    with eng.Fori(1, PREP_AT) as blk:
                        rest(base + blk, par, blk, None)
                    with eng.Fori(PREP_AT, BLOCKS) as blk:
                        rest(base + blk, par, blk, ((pair * (2 * WT) + (par + 1) * WT) + (blk - PREP_AT),
                                                    pair * 2 + (par + 2)))

        @block.sync
        def _(sp):
            sp.nop().then_inc(s["v_stacked"], FREE_DMA)
            sp.nop().then_inc(s["out_done"], FREE_DMA)
            sp.dma_start(wffn_q, q_ffn.rearrange("(c p) e -> p c e", p=P)).then_inc(s["ffnw_in"], 16)
            sp.dma_start(wbase_n, w_base.rearrange("(c p) e -> p c e", p=P)).then_inc(s["ffnw_in"], 16)
            sp.dma_start(lorab_n, lora_b.rearrange("(c p) r -> p c r", p=P)).then_inc(s["ffnw_in"], 16)

            def load_weights(par, kv):
                q = w_qkv[bass.ds(kv * (G * D), G * D), :] if not isinstance(kv, int) else w_qkv[kv * G * D:(kv + 1) * G * D, :]
                k = w_qkv[bass.ds(kv * D + HEADS * D, D), :]
                v = w_qkv[bass.ds(kv * D + (HEADS + KV) * D, D), :]
                d = w_dense[:, bass.ds(kv * (G * D), G * D)]
                sp.dma_start(WN[par][:, 0:G, :], q.rearrange("(g p) e -> p g e", p=P)).then_inc(s["wn_in"], 16)
                sp.dma_start(WN[par][:, KT, :], k).then_inc(s["wn_in"], 16)
                sp.dma_start(WN[par][:, VT, :], v).then_inc(s["wn_in"], 16)
                sp.dma_start(WN[par][:, DT:WT, :], d.rearrange("(c p) e -> p c e", p=P)).then_inc(s["wn_in"], 16)

            load_weights(0, 0)
            for n in range(4):
                sp.dma_start(X2[:, 8 * n:8 * n + 8, :], x_t[:, 8 * n:8 * n + 8, :]).then_inc(s["x_in"], 16)

            def stack_values(i):
                sp.wait_ge(s["v_lo"], i + 1 + FREE)
                sp.wait_ge(s["a_done"], i * 2 + 2)
                for a in range(TB):
                    for j in range(4):
                        sp.dma_start(VST[j * S:(j + 1) * S, a::TB, :],
                                     VHL[a * S:(a + 1) * S, :, j // 2, :]).then_inc(s["v_stacked"], 16)

            def first(i, par, pair):
                stack_values(i)
                sp.wait_ge(s["x2_done"], i * 2 + 2 + FREE)
                if par == 0:
                    sp.wait_ge(s["c_lo"], TILES)
                load_weights(1 - par, pair * 2 + 1 if par == 0 else (pair * 2 + 2) % KV)

            def rest(i, par, blk, prep):
                stack_values(i)

            steps(sp, first, rest)
            with sp.Fori(0, TILES // 2) as pair:
                for n in range(2):
                    sp.wait_ge(s["ot_ready"], pair * 2 + n + 1 + FREE)
                    sp.dma_start(out_t[pair * 2 + n, :, :], OT[n]).then_inc(s["out_done"], 16)
            sp.wait_ge(s["out_done"], 16 * TILES + FREE_DMA)

        @block.gpsimd
        def _(pool):
            pool.dma_start(cidx[:, :], cond_index.rearrange("(b o) -> b o", o=1)).then_inc(s["cond_in"], 16)
            pool.wait_ge(s["cond_in"], 16)
            pool.indirect_dma_start(gath, None, w_cond.rearrange("n c d -> n (c d)"),
                                    bass.IndirectOffsetOnAxis(ap=cidx[:, 0:1], axis=0)).then_inc(s["gath_in"], 16)
            turns = [0]

            def turn(ins):
                turns[0] += 1
                ins.then_inc(s["pool_turn"], 1)
                pool.wait_ge(s["pool_turn"], turns[0])

            pool.wait_ge(s["gath_in"], 16)
            turn(pool.memset(wn1, 0.0))
            turn(pool.memset(ident[:, :], 0.0))
            turn(pool.affine_select(out=ident[:, :], in_=ident[:, :], compare_op=ALU.not_equal, fill=1.0, base=0,
                                    pattern=[[-1, P]], channel_multiplier=1))
            turn(pool.tensor_copy(ident16[:, :], ident[:, :]))
            assert turns[0] == IDENTS_TURN
            turn(pool.memset(mask[:, :], 0.0))
            for q in range(4):
                m = mask[q * S:(q + 1) * S, :]
                turn(pool.affine_select(out=m, in_=m, compare_op=ALU.is_ge, fill=1.0, base=0,
                                        pattern=[[-1, S]], channel_multiplier=1))
            turn(pool.tensor_scalar(mask[:, :], mask[:, :], MASKED, None, ALU.mult))
            turn(pool.memset(PST[:, :, :, :], 0.0))
            turn(pool.memset(VST[:, :, :], 0.0))
            turn(pool.memset(wsc[1][:, :], 0.0))
            assert turns[0] == POOL_TURNS

            def stage_tile(par, r, n):
                if not (isinstance(n, int) and n == 0):
                    pool.wait_ge(s["w_t"], n)
                src = WN[par][:, r, :] if isinstance(r, int) else \
                    WN[par][:, bass.ds(r, 1), :].rearrange("p o e -> p (o e)")
                pool.tensor_copy(ST[:, :], src).then_inc(s["stage_full"], 1)

            pool.wait_ge(s["wn_in"], 64)
            stage_tile(0, 0, 0)
            pool.wait_ge(s["stage_full"], 1)
            pool.wait_ge(s["wmax_ready"], 2)
            pool.partition_all_reduce(wsc[0][:, 0:2], wsc[0][:, 6:8], P, RED.absmax).then_inc(s["wmax_all"], 1)
            pool.wait_ge(s["wmax_all"], 1)
            for r in range(1, WT):
                stage_tile(0, r, r)
            pool.wait_ge(s["xmax_ready"], 1)
            pool.partition_all_reduce(bounds[:, 0:2], xmaxs[:, 8:10], P, RED.absmax).then_inc(s["xmax_all"], 1)
            pool.wait_ge(s["xmax_all"], 1)
            pool.wait_ge(s["c_done"], TILES)
            pool.memset(WN[1][:, DT:WT, :], 0.0).then_inc(s["dense_zeroed"], 1)
            pool.wait_ge(s["dense_zeroed"], 1)

            for kv in range(KV):
                sc = wsc[(kv + 1) % 2]
                pool.wait_ge(s["wmax_ready"], 2 * (kv + 2))
                pool.partition_all_reduce(sc[:, 0:2], sc[:, 6:8], P, RED.absmax).then_inc(s["wmax_all"], 1)
                pool.wait_ge(s["wmax_all"], kv + 2)
                with pool.Fori(0, WT) as r:
                    stage_tile((kv + 1) % 2, r, (kv + 1) * WT + r)

        @block.scalar
        def _(act):
            act.dma_start(label[:, :, :].rearrange("p n a -> p (n a)"),
                          label_index.rearrange("(o b) -> o b", o=1).to_broadcast([P, B])).then_inc(s["small_in"], 16)
            act.dma_start(fsc[:, 0:1], ffn_scale.rearrange("(o n) -> o n", o=1).to_broadcast([P, 1])).then_inc(s["small_in"], 16)
            act.dma_start(fsc[:, 1:2], ffn_zero.rearrange("(o n) -> o n", o=1).to_broadcast([P, 1])).then_inc(s["small_in"], 16)
            act.dma_start(LB[R:R + 1, :], ffn_bias.rearrange("(o n) -> o n", o=1)).then_inc(s["small_in"], 16)
            act.dma_start(wcond_n, w_cond.rearrange("n c d -> (n c d)").rearrange("(p f) -> p f", p=P)).then_inc(s["small_in"], 16)
            for c in range(NC):
                act.dma_start(LA[:, c, :, :], lora_a[:, c * P:(c + 1) * P, :].rearrange("l p r -> p l r")).then_inc(s["small_in"], 16)
            act.wait_ge(s["gath_in"], 16)
            act.dma_start(gathered, gath).then_inc(s["gath_out"], 16)
            act.wait_ge(s["gath_out"], 16)
            act.wait_ge(s["pool_turn"], 1)
            src = gathered.rearrange("(n a) (c d) -> a c n d", a=TB, c=S)
            for a in range(TB):
                act.dma_start(bd[a * S:(a + 1) * S, :, a * S:(a + 1) * S], src[a]).then_inc(s["bd_in"], 16)

            for c in range(NC):
                act.wait_ge(s["ffn_t"], c + 1)
                act.activation(wffn_t[:, :, c * P:(c + 1) * P], chunks(pQ[c % 2][:, :]), ACT.Copy).then_inc(s["ffn_tc"], 1)
            for c in range(NC):
                act.wait_ge(s["m_done"], c + 1)
                act.activation(M[:, c, :], pA[c % 2][:, :], ACT.Copy).then_inc(s["m_copied"], 1)
            act.wait_ge(s["m_done"], NC + 1)
            act.activation(LB[0:R, :], pD[0:R, :], ACT.Copy, scale=0.5).then_inc(s["m_copied"], 1)

            def weight_hi(par, r, n):
                act.wait_ge(s["w_t"], n + 1)
                act.activation(half_of(par, r, 0), chunks(pA[1][:, :]), ACT.Copy,
                               scale=wts[par][:, bass.ds(r, 1)]).then_inc(s["w_hi"], 1)

            act.wait_ge(s["wscale_ready"], 1)
            with act.Fori(0, WT) as r:
                weight_hi(0, r, r)
            act.wait_ge(s["cscale_ready"], 1)
            with act.Fori(0, TILES // 2) as pair:
                for m in range(2):
                    n = pair * 2 + m
                    act.wait_ge(s["c_done"], n + 1)
                    act.activation(CH[:, :, bass.ds(n * P, P)], chunks(pQ[m][:, :]), ACT.Copy,
                                   scale=bounds[:, 6:7]).then_inc(s["c_hi"], 1)

            def project(i, par, blk, prep):
                if prep is not None:
                    act.wait_ge(s["wscale_ready"], prep[1])
                    weight_hi(1 - par, blk - PREP_AT, prep[0])
                act.wait_ge(s["k_done"], i + 1)
                act.activation(KHL[:, :, 0, :], pKV[:, 0:BT].rearrange("p (b t) -> p b t", b=BB), ACT.Copy,
                               scale=EVAC).then_inc(s["k_hi"], 1)
                for n in range(2):
                    act.wait_ge(s["q_done"], i * 2 + (n + 1))
                    act.activation(two_heads(QH, n), pQ[n][:, :].rearrange("p (b n) -> p b n", b=BB),
                                   ACT.Copy, scale=EVAC).then_inc(s["q_hi"], 1)

            def attend(i):
                act.wait_ge(s["t_done"], i + 1)
                act.activation(PT[:, :, :], pT16[:, :].rearrange("p (b t) -> p b t", b=BB), ACT.Copy
                               ).then_inc(s["pt_copied"], 1)

            def values(i):
                act.wait_ge(s["v_done"], i + 1)
                act.wait_ge(s["v_stacked"], i * (16 * VDMAS) + FREE_DMA)
                act.activation(VHL[:, :, 0, :], pKV[:, BT:BT + BTILES * D].rearrange("p (n d) -> p n d", n=BTILES),
                               ACT.Copy, scale=EVAC).then_inc(s["v_hi"], 1)

            def attended(i):
                for n in range(2):
                    act.wait_ge(s["a_done"], i * 2 + (n + 1))
                    act.activation(AH[:, :, n * P:(n + 1) * P], pA[n][:, :].rearrange("p (g n) -> p g n", g=G),
                                   ACT.Copy).then_inc(s["a_hi"], 1)

            def softmax(i, par):
                act.wait_ge(s["s_sub"], i + 1)
                act.activation(S2[:, :, :], S1[:, :, :], ACT.Exp, scale=wsc[par][:, 9:10]).then_inc(s["exp_done"], 1)
                act.wait_ge(s["p_full"], i + 1)
                act.activation(PST[:, :, 0::2, :], PR[:, :, :].unsqueeze(2).to_broadcast([P, BB, 2, S]),
                               ACT.Copy).then_inc(s["p_hi"], 1)

            def step(i, par, blk, prep):
                project(i, par, blk, prep)
                attend(i)
                values(i)
                attended(i)
                softmax(i, par)

            act.wait_ge(s["pool_turn"], POOL_TURNS)
            steps(act, lambda i, par, pair: step(i, par, 0, None), step)
            attend(KV * BLOCKS)
            attended(KV * BLOCKS)

            act.wait_ge(s["x2_done"], 2 * (KV * BLOCKS + 1) + FREE)
            act.wait_ge(s["one_ready"], 2)
            with act.Fori(0, TILES // 2) as pair:
                for m in range(2):
                    n = pair * 2 + m
                    act.wait_ge(s["ot_ready"], n - m + FREE)
                    act.activation(XS[m], X2[:, bass.ds(n, 1), :].rearrange("p o e -> p (o e)"),
                                   ACT.Copy).then_inc(s["xs_ready"], 1)
                for m in range(2):
                    act.wait_ge(s["xt_t"], pair * 2 + (m + 1))
                    act.activation(XT[m], chunks(pQ[m][:, :]), ACT.Copy).then_inc(s["xt_copied"], 1)
                for m in range(2):
                    act.wait_ge(s["low_t"], pair * 2 + (m + 1))
                    act.activation(LOWT[m][0:R, :], [pKV, pT][m][0:R, 0:P], ACT.Copy).then_inc(s["lowt_copied"], 1)

        @block.vector
        def _(dve):
            def chained(instructions, base):
                n = 0
                for ins in instructions:
                    n += 1
                    ins.then_inc(s["chain"], 1)
                    dve.wait_ge(s["chain"], base + n)
                return n

            def powers(src, power, inverse):
                yield dve.tensor_scalar(power, src, 1e-30, 2.0, ALU.max, ALU.mult)
                yield dve.tensor_scalar(power.bitcast(i32), power.bitcast(i32), 0x7F800000, None, ALU.bitwise_and)
                yield dve.tensor_scalar(inverse.bitcast(i32), power.bitcast(i32), -1.0, float(254 << 23),
                                        ALU.mult, ALU.add)

            def max_pair(par, k):
                src = WN[par][:, bass.ds(k * 2, 2), :].rearrange("p r e -> p (r e)")
                dve.tensor_reduce(wmaxs[:, bass.ds(k, 1)], src, AX.X, ALU.max, apply_absolute_value=True
                                  ).then_inc(s["wmax_part"], 1)

            def head_max(par, n):
                dve.wait_ge(s["wmax_part"], n)
                dve.tensor_reduce(wsc[par][:, 6:7], wmaxs[:, 0:DT // 2], AX.X, ALU.max).then_inc(s["wmax_ready"], 1)
                dve.tensor_reduce(wsc[par][:, 7:8], wmaxs[:, DT // 2:WT // 2], AX.X, ALU.max).then_inc(s["wmax_ready"], 1)

            def tile_scales(par):
                sc = wsc[par]
                yield from powers(sc[:, 0:2], sc[:, 2:4], sc[:, 4:6])
                for k, (lo, hi) in enumerate(((0, DT), (DT, WT))):
                    ins = dve.tensor_scalar(wts[par][:, lo:hi], sc[:, 4 + k:5 + k].to_broadcast([P, hi - lo]),
                                            SPLIT, None, ALU.mult)
                    yield ins

            def stage_scales(par):
                sc = wsc[par]
                yield dve.tensor_scalar(sc[:, 8:9], sc[:, 2:3], bounds[:, 4:5], E / SPLIT, ALU.mult, ALU.mult)
                yield dve.scalar_tensor_tensor(sc[:, 9:10], sc[:, 8:9], float(D) ** -0.5, sc[:, 8:9],
                                               ALU.mult, ALU.mult)
                yield dve.tensor_scalar(sc[:, 10:11], sc[:, 3:4], sc[:, 8:9], 1.0 / SPLIT, ALU.mult, ALU.mult)

            for name in "v_lo q_lo p_lo x2_done a_lo s_read w_lo ot_ready".split():
                dve.nop().then_inc(s[name], FREE)
            dve.wait_ge(s["ffnw_in"], 48)
            dve.wait_ge(s["small_in"], 16 * (5 + NC))
            dve.tensor_scalar(wffn_f, wffn_q, fsc[:, 1:2], fsc[:, 0:1], ALU.subtract, ALU.mult).then_inc(s["ffn_ready"], 1)
            dve.tensor_reduce(xmaxs[:, 9:10], wcond_n, AX.X, ALU.max, apply_absolute_value=True).then_inc(s["chain"], 1)
            for l in range(NLAB):
                for a in range(TB):
                    dve.tensor_scalar(onehot[a * S:(a + 1) * S, :, l], label[a * S:(a + 1) * S, :, a], float(l), None,
                                      ALU.is_equal).then_inc(s["onehot_ready"], 1)

            def weight_lo(par, r, n):
                dve.wait_ge(s["w_hi"], n + 1)
                dve.scalar_tensor_tensor(half_of(par, r, 1), chunks(pA[1][:, :]), wts[par][:, bass.ds(r, 1)],
                                         half_of(par, r, 0), ALU.mult, ALU.subtract).then_inc(s["w_lo"], 1)

            dve.wait_ge(s["wn_in"], 64)
            for k in range(WT // 2):
                max_pair(0, k)
            head_max(0, WT // 2)
            dve.wait_ge(s["wmax_all"], 1)
            n_tiles = chained(tile_scales(0), 1)
            dve.tensor_copy(wsc[0][:, 11:12], wts[0][:, 0:1]).then_inc(s["wscale_ready"], 1)
            with dve.Fori(0, WT) as r:
                weight_lo(0, r, r)
            for n in range(4):
                dve.wait_ge(s["x_in"], 64)
                for m in range(2):
                    dve.tensor_reduce(xmaxs[:, 2 * n + m:2 * n + m + 1],
                                      X2[:, 8 * n + 4 * m:8 * n + 4 * m + 4, :].rearrange("p n e -> p (n e)"),
                                      AX.X, ALU.max, apply_absolute_value=True).then_inc(s["chain"], 1)
            dve.wait_ge(s["chain"], n_tiles + 9)
            dve.tensor_reduce(xmaxs[:, 8:9], xmaxs[:, 0:8], AX.X, ALU.max).then_inc(s["xmax_ready"], 1)

            def c_scale():
                yield from powers(bounds[:, 0:2], bounds[:, 2:4], xmaxs[:, 0:2])
                yield dve.tensor_scalar(bounds[:, 4:5], bounds[:, 2:3], bounds[:, 3:4], float(S), ALU.mult, ALU.mult)
                yield dve.tensor_scalar(bounds[:, 5:6].bitcast(i32), bounds[:, 4:5].bitcast(i32), -1.0,
                                        float(254 << 23), ALU.mult, ALU.add)

            dve.wait_ge(s["xmax_all"], 1)
            n_c = chained(c_scale(), n_tiles + 9)
            dve.tensor_scalar(bounds[:, 6:7], bounds[:, 5:6], SPLIT, None, ALU.mult).then_inc(s["cscale_ready"], 1)
            n_stage = chained(stage_scales(0), n_tiles + 9 + n_c)
            dve.wait_ge(s["cscale_ready"], 1)
            used, per_head = n_tiles + 9 + n_c + n_stage, n_tiles + n_stage
            with dve.Fori(0, TILES // 2) as pair:
                for m in range(2):
                    n = pair * 2 + m
                    dve.wait_ge(s["c_hi"], n + 1)
                    dve.scalar_tensor_tensor(CL[:, :, bass.ds(n * P, P)], chunks(pQ[m][:, :]), bounds[:, 6:7],
                                             CH[:, :, bass.ds(n * P, P)], ALU.mult, ALU.subtract).then_inc(s["c_lo"], 1)

            def low(out, psum, high, done, scale=EVAC):
                dve.scalar_tensor_tensor(out, psum, scale, high, ALU.mult, ALU.subtract).then_inc(s[done], 1)

            def project(i, par, blk, prep):
                if prep is not None:
                    weight_lo(1 - par, blk - PREP_AT, prep)
                dve.wait_ge(s["k_hi"], i + 1)
                low(KHL[:, :, 1, :], pKV[:, 0:BT].rearrange("p (b t) -> p b t", b=BB), KHL[:, :, 0, :], "k_lo")
                for n in range(2):
                    dve.wait_ge(s["q_hi"], i * 2 + (n + 1))
                    low(two_heads(QL, n), pQ[n][:, :].rearrange("p (b n) -> p b n", b=BB), two_heads(QH, n), "q_lo")

            def values(i):
                dve.wait_ge(s["v_hi"], i + 1)
                low(VHL[:, :, 1, :], pKV[:, BT:BT + BTILES * D].rearrange("p (n d) -> p n d", n=BTILES),
                    VHL[:, :, 0, :], "v_lo")

            def attended(i):
                for n in range(2):
                    dve.wait_ge(s["a_hi"], i * 2 + (n + 1))
                    low(AL[:, :, n * P:(n + 1) * P], pA[n][:, :].rearrange("p (g n) -> p g n", g=G),
                        AH[:, :, n * P:(n + 1) * P], "a_lo", 1.0)

            def spread(row):
                return row.unsqueeze(2).to_broadcast([P, BB, S])

            def scores(i, base):
                dve.wait_ge(s["s_done"], i + 1)
                sc = pS[:, :].rearrange("p (b h t) -> p b h t", b=BB, h=2)
                chained([dve.tensor_tensor(S1[:, :, :], sc[:, :, 0, :],
                                           mask[:, :].unsqueeze(1).to_broadcast([P, BB, S]), ALU.add)], base)
                dve.tensor_tensor(S2[:, :, :], S1[:, :, :], sc[:, :, 1, :], ALU.add).then_inc(s["s_read"], 1)
                dve.wait_ge(s["s_read"], i + 1 + FREE)
                chained([dve.tensor_reduce(smax[:, :], S2[:, :, :], AX.X, ALU.max)], base + 1)
                dve.tensor_tensor(S1[:, :, :], S2[:, :, :], spread(smax[:, :]), ALU.subtract).then_inc(s["s_sub"], 1)

            def probabilities(i, base):
                dve.wait_ge(s["exp_done"], i + 1)
                chained([dve.tensor_reduce(ssum[:, :], S2[:, :, :], AX.X, ALU.add)], base)
                chained([dve.reciprocal(srec[:, :], ssum[:, :])], base + 1)
                dve.tensor_tensor(PR[:, :, :], S2[:, :, :], spread(srec[:, :]), ALU.mult).then_inc(s["p_full"], 1)
                dve.wait_ge(s["p_hi"], i + 1)
                dve.tensor_tensor(PST[:, :, 1::2, :], PR[:, :, :].unsqueeze(2).to_broadcast([P, BB, 2, S]),
                                  PST[:, :, 0::2, :], ALU.subtract).then_inc(s["p_lo"], 1)

            def update(i, par, tile, n):
                dve.wait_ge(s["d_done"], i * 2 + (n + 1))
                t = X2[:, bass.ds(tile, 1), :].rearrange("p o e -> p (o e)")
                dve.scalar_tensor_tensor(t, [pD, pT][n][:, :], wsc[par][:, 10:11], t, ALU.mult, ALU.add
                                         ).then_inc(s["x2_done"], 1)

            PER = 4

            def step(i, par, before, blk, prep, tile, head, loads=None):
                base = i * PER + head + used
                project(i, par, blk, prep)
                values(i)
                attended(i)
                scores(i, base)
                update(i, before, tile, 0)
                probabilities(i, base + 2)
                update(i, before, tile + 1, 1)
                if prep is None and not isinstance(blk, int):
                    dve.wait_ge(s["wn_in"], loads)
                    max_pair(1 - par, blk - 1)

            last_tile = (BLOCKS - 1) * BTILES
            dve.wait_ge(s["pool_turn"], POOL_TURNS)
            with dve.Fori(0, KV // 2) as pair:
                for par in range(2):
                    start = pair * (2 * BLOCKS) + par * BLOCKS
                    prep = pair * (2 * WT) + (par + 1) * WT
                    head = pair * (2 * per_head) + par * per_head
                    step(start, par, 1 - par, 0, None, last_tile, head)
                    with dve.Fori(1, PREP_AT) as blk:
                        step(start + blk, par, par, blk, None, (blk - 1) * BTILES, head, pair * 128 + (par + 2) * 64)
                    head_max(1 - par, (pair * WT + (par + 2) * (WT // 2)))
                    dve.wait_ge(s["wmax_all"], pair * 2 + (par + 2))
                    base = (start + PREP_AT) * PER + head + used
                    chained(tile_scales(1 - par), base)
                    chained(stage_scales(1 - par), base + n_tiles)
                    dve.tensor_copy(wsc[1 - par][:, 11:12], wts[1 - par][:, 0:1]).then_inc(s["wscale_ready"], 1)
                    with dve.Fori(PREP_AT, BLOCKS) as blk:
                        step(start + blk, par, par, blk, prep + (blk - PREP_AT), (blk - 1) * BTILES, head + per_head)
            attended(KV * BLOCKS)
            for n in range(2):
                update(KV * BLOCKS, 1, last_tile + n, n)

            dve.wait_ge(s["x2_done"], 2 * (KV * BLOCKS + 1) + FREE)
            for m in range(2):
                dve.memset(LOWT[m][R:R + 1, :], 1.0).then_inc(s["one_ready"], 1)
            done = KV * BLOCKS * PER + used + KV * per_head
            with dve.Fori(0, TILES // 2) as pair:
                for m in range(2):
                    n = pair * 2 + m
                    dve.wait_ge(s["low_done"], n + 1)
                    which = onehot[:, bass.ds(n, 1), :].rearrange("p o l -> p (o l)").unsqueeze(2).to_broadcast([P, NLAB, R])
                    chained([dve.tensor_tensor(LOWM, [pS, pD][m][:, 0:NLAB * R].rearrange("p (l r) -> p l r", l=NLAB),
                                               which, ALU.mult)], n + done)
                    dve.tensor_reduce(LOW[m], LOWM.rearrange("p l r -> p r l"), AX.X, ALU.add
                                      ).then_inc(s["low_sel"], 1)
                    dve.wait_ge(s["low_sel"], n + 1)
                for m in range(2):
                    n = pair * 2 + m
                    dve.wait_ge(s["y_done"], n + 1)
                    dve.wait_ge(s["out_done"], pair * 32 + FREE_DMA)
                    dve.tensor_tensor(OT[m], pA[m][:, :], XS[m], ALU.add).then_inc(s["ot_ready"], 1)

        @block.tensor
        def _(pe):
            mm = nc.tensor.matmul
            pe.wait_ge(s["pool_turn"], IDENTS_TURN)
            pe.wait_ge(s["ffn_ready"], 1)
            for oc in range(NC):
                if oc >= 2:
                    pe.wait_ge(s["ffn_tc"], oc - 1)
                for mc in range(NC):
                    last = nc.tensor.transpose(pQ[oc % 2][:, mc * P:(mc + 1) * P],
                                               wffn_f[:, oc, mc * P:(mc + 1) * P], ident[:, :])
                last.then_inc(s["ffn_t"], 1)
            pe.wait_ge(s["ffn_tc"], NC)
            for ic in range(NC):
                if ic >= 2:
                    pe.wait_ge(s["m_copied"], ic - 1)
                for mc in range(NC):
                    last = mm(pA[ic % 2][:, :], wbase_n[:, mc, ic * P:(ic + 1) * P], wffn_t[:, mc, :],
                              start=(mc == 0), stop=(mc == NC - 1))
                last.then_inc(s["m_done"], 1)
            for mc in range(NC):
                last = mm(pD[0:R, :], lorab_n[:, mc, :], wffn_t[:, mc, :], start=(mc == 0), stop=(mc == NC - 1))
            last.then_inc(s["m_done"], 1)
            pe.wait_ge(s["m_copied"], NC)

            def weight_tile(n, first=False):
                pe.wait_ge(s["stage_full"], n + 1)
                if first:
                    pe.wait_ge(s["w_lo"], n + FREE)
                for c in range(NC):
                    last = nc.tensor.transpose(pA[1][:, c * P:(c + 1) * P], ST[:, c * P:(c + 1) * P], ident[:, :])
                last.then_inc(s["w_t"], 1)

            with pe.Fori(0, WT) as r:
                weight_tile(r, True)
            pe.wait_ge(s["bd_in"], 16 * TB)
            pe.wait_ge(s["x_in"], 64)
            for n in range(TILES):
                if n >= 2:
                    pe.wait_ge(s["c_lo"], n - 1)
                for c in range(NC):
                    last = mm(pQ[n % 2][:, c * P:(c + 1) * P], X2[:, n, c * P:(c + 1) * P], bd[:, n, :],
                              start=True, stop=True)
                last.then_inc(s["c_done"], 1)
            pe.wait_ge(s["c_lo"], TILES)

            HL = ((0, 0), (0, 1), (1, 0))

            def half(h, c, lo, n):
                return (CH, CL)[h][:, c, bass.ds(lo, n)]

            def project(i, par, blk, prep):
                if prep is not None:
                    weight_tile(prep[0])
                pe.wait_ge(s["v_lo"], i + FREE)
                for c in range(NC):
                    for w, h in HL:
                        last = mm(pKV[:, 0:BT], WH[par][:, KT, w, c, :], half(h, c, blk * BT, BT),
                                  start=(c == 0 and w + h == 0), stop=(c == NC - 1 and w == 1))
                last.then_inc(s["k_done"], 1)
                pe.wait_ge(s["q_lo"], i * 2 + FREE)
                for g in range(G):
                    for c in range(NC):
                        for w, h in HL:
                            last = mm(pQ[g // 2][:, :].rearrange("p (b g t) -> p b g t", b=BB, g=2)[:, :, g % 2, :],
                                      WH[par][:, g, w, c, :],
                                      half(h, c, blk * BT, BT).rearrange("p (b t) -> p b t", b=BB),
                                      start=(c == 0 and w + h == 0), stop=(c == NC - 1 and w == 1))
                    if g % 2:
                        last.then_inc(s["q_done"], 1)

            def transposes(i):
                pe.wait_ge(s["p_lo"], i + FREE)
                pe.wait_ge(s["x2_done"], i * 2 + FREE)
                for b in range(BB):
                    last = nc.tensor.transpose(pT16[:, b * P:(b + 1) * P],
                                               PST[:, b, :, :].rearrange("p h t -> p (h t)"), ident16[:, :])
                last.then_inc(s["t_done"], 1)

            def values(i, par, blk):
                pe.wait_ge(s["k_lo"], i + 1)
                for n in range(BTILES):
                    for c in range(NC):
                        for h, w in HL:
                            last = mm(pKV[:, BT + n * D:BT + (n + 1) * D], half(h, c, blk * BT + n * P, P),
                                      WH[par][:, VT, w, c, :],
                                      start=(c == 0 and w + h == 0), stop=(c == NC - 1 and h == 1))
                last.then_inc(s["v_done"], 1)

            def attend(i, tiles_done):
                pe.wait_ge(s["v_stacked"], i * (16 * VDMAS) + FREE_DMA)
                pe.wait_ge(s["pt_copied"], i + 1)
                pe.wait_ge(s["a_lo"], i * 2 + FREE)
                if tiles_done is not None:
                    pe.wait_ge(s["w_lo"], tiles_done + FREE)
                for b in range(BB):
                    last = mm(pA[b // TB][:, :].rearrange("p (g b t) -> p b g t", g=G, b=TB)[:, b % TB, :, :],
                              VST[:, b, :], PT[:, b, :].rearrange("p (g t) -> p g t", g=G),
                              start=True, stop=True)
                    if b % TB == TB - 1:
                        last.then_inc(s["a_done"], 1)

            def scores(i):
                pe.wait_ge(s["k_lo"], i + 1)
                pe.wait_ge(s["q_lo"], i * 2 + 2 + FREE)
                pe.wait_ge(s["s_read"], i + FREE)
                for b in range(BB):
                    q = [h[:, b, :, :].rearrange("p g t -> p (g t)") for h in (QH, QL)]
                    mm(pS[:, b * 2 * S:(b + 1) * 2 * S], q[0], KHL[:, b, :, :].rearrange("p h t -> p (h t)"),
                       start=True, stop=False)
                    last = mm(pS[:, b * 2 * S:b * 2 * S + S], q[1], KHL[:, b, 0, :], start=False, stop=True)
                last.then_inc(s["s_done"], 1)

            def dense(i, par):
                for n in range(BTILES):
                    pe.wait_ge(s["a_lo"], i * 2 + (n + 1) + FREE)
                    for g in range(G):
                        for a, w in HL:
                            last = mm([pD, pT][n][:, :], (AH, AL)[a][:, g, n * P:(n + 1) * P],
                                      WH[par][:, DT:WT, w, g, :],
                                      start=(g == 0 and a + w == 0), stop=(g == G - 1 and a == 1))
                    last.then_inc(s["d_done"], 1)

            def step(i, par, before, blk, prep):
                project(i, par, blk, prep)
                transposes(i)
                values(i, par, blk)
                attend(i, None if prep is None else prep[0] + 1)
                scores(i)
                dense(i, before)

            def first(i, par, pair):
                pe.wait_ge(s["w_lo"], pair * (2 * WT) + (par + 1) * WT + FREE)
                step(i, par, 1 - par, 0, None)

            pe.wait_ge(s["pool_turn"], POOL_TURNS)
            pe.wait_ge(s["dense_zeroed"], 1)
            steps(pe, first, lambda i, par, blk, prep: step(i, par, par, blk, prep))
            end = KV * BLOCKS
            transposes(end)
            attend(end, None)
            dense(end, 1)

            low_bank, lowt_bank = (pS, pD), (pKV, pT)
            with pe.Fori(0, TILES // 2) as pair:
                for m in range(2):
                    n = pair * 2 + m
                    pe.wait_ge(s["xs_ready"], n + 1)
                    for c in range(NC):
                        last = nc.tensor.transpose(pQ[m][:, c * P:(c + 1) * P], XS[m][:, c * P:(c + 1) * P], ident[:, :])
                    last.then_inc(s["xt_t"], 1)
                for m in range(2):
                    n = pair * 2 + m
                    pe.wait_ge(s["xt_copied"], n + 1)
                    for c in range(NC):
                        last = mm(low_bank[m][:, 0:NLAB * R], XT[m][:, c, :], LA[:, c, :, :].rearrange("p l r -> p (l r)"),
                                  start=(c == 0), stop=(c == NC - 1))
                    last.then_inc(s["low_done"], 1)
                    pe.wait_ge(s["ot_ready"], n - m + FREE)
                    for c in range(NC):
                        mm(pA[m][:, :], XT[m][:, c, :], M[:, c, :], start=(c == 0), stop=False)
                for m in range(2):
                    n = pair * 2 + m
                    pe.wait_ge(s["low_sel"], n + 1)
                    nc.tensor.transpose(lowt_bank[m][0:R, 0:P], LOW[m], ident[:, :]).then_inc(s["low_t"], 1)
                for m in range(2):
                    n = pair * 2 + m
                    pe.wait_ge(s["lowt_copied"], n + 1)
                    mm(pA[m][:, :], LOWT[m], LB[:, :], start=False, stop=True).then_inc(s["y_done"], 1)


_INS = ["x", "itok_B_0_15", "itok_B_0_2", "L0_cond_weights", "L0_attn_w_qkv", "L0_attn_w_dense", "L0_cond2_W",
        "L0_cond2_lora_A", "L0_cond2_lora_B_w", "L0_ffn_qweight", "L0_ffn_scale", "L0_ffn_zero_point", "L0_ffn_bias"]


def kernel(**inputs):
    import numpy as np
    import concourse.bacc as bacc
    from concourse.bass_utils import run_bass_kernel_spmd

    nc = bacc.Bacc("TRN2", target_bir_lowering=False, num_devices=1)
    arrays, args = {}, []
    for name in _INS:
        a = np.ascontiguousarray(inputs[name])
        arrays[f"in_{name}"] = a
        args.append(nc.dram_tensor(f"in_{name}", a.shape, mybir.dt.from_np(a.dtype), kind="ExternalInput").ap())
    shape = inputs["x"].shape
    args.append(nc.dram_tensor("out", shape, mybir.dt.float32, kind="ExternalOutput").ap())
    adaln_attention_ffn_kernel(nc, *args)
    r = run_bass_kernel_spmd(nc, [arrays], core_ids=[0])
    return r.results[0]["out"]
```

```python
from contextlib import ExitStack

import concourse.bass as bass
from concourse import mybir
from concourse.alu_op_type import AluOpType as ALU


def adaln_attention_ffn_kernel(
    nc: bass.Bass,
    x: bass.AP,
    cond_index: bass.AP,
    label_index: bass.AP,
    w_cond: bass.AP,
    w_qkv: bass.AP,
    w_dense: bass.AP,
    w_base: bass.AP,
    lora_a: bass.AP,
    lora_b: bass.AP,
    q_ffn: bass.AP,
    ffn_scale: bass.AP,
    ffn_zero: bass.AP,
    ffn_bias: bass.AP,
    out: bass.AP,
):
    f32, f16, i32 = mybir.dt.float32, mybir.dt.float16, mybir.dt.int32
    ACT = mybir.ActivationFunctionType
    AX = mybir.AxisListType
    RED = bass.bass_isa.ReduceOp

    P = 128
    B, S, E = x.shape
    NCOND = w_cond.shape[0]
    NLAB, _, R = lora_a.shape
    HEADS, KV, D = 32, 8, 128
    G = HEADS // KV
    NC = E // P
    TOK = B * S
    TILES = TOK // P
    TB = P // S
    BB = 8
    BT = BB * S
    BTILES = BT // P
    BLOCKS = B // BB
    WT = G + 2 + NC
    KT, VT, DT = G, G + 1, G + 2
    PREP_AT = BLOCKS - WT
    VDMAS = TB * 4

    IDENTS_TURN, POOL_TURNS = 3, 13
    SPLIT = 2.0 ** 15
    EVAC = 2.0 ** -24
    MASKED = -3.0e38

    x_t = x.rearrange("(n a) s e -> (a s) n e", a=TB)
    out_t = out.rearrange("(n a) s e -> n (a s) e", a=TB)
    gathered = nc.dram_tensor("gathered", [B, S * S], f32, kind="Internal").ap()

    ctx = ExitStack()
    with ctx:
        def sb(name, shape, dt=f32):
            return ctx.enter_context(nc.sbuf_tensor(name, shape, dt))

        def pb(name, shape, dt=f32):
            return ctx.enter_context(nc.psum_tensor(name, shape, dt))

        def sem(name):
            return ctx.enter_context(nc.semaphore(name))

        X2 = sb("X2", [P, TILES, E])
        CH = sb("CH", [P, NC, TOK], f16)
        CL = sb("CL", [P, NC, TOK], f16)
        WN = [sb(f"WN{p}", [P, WT, E]) for p in range(2)]
        WH = [w[:, :, :].bitcast(f16).rearrange("p r (h c d) -> p r h c d", h=2, c=NC) for w in WN]
        ST = sb("ST", [P, E])
        QH = sb("QH", [P, BB, G, S], f16)
        QL = sb("QL", [P, BB, G, S], f16)
        KHL = sb("KHL", [P, BB, 2, S], f16)
        VHL = sb("VHL", [P, BTILES, 2, D], f16)
        VST = sb("VST", [P, BB, D], f16)
        PST = sb("PST", [P, BB, 4, S], f16)
        PT = sb("PT", [P, BB, P], f16)
        AH = sb("AH", [P, G, BT], f16)
        AL = sb("AL", [P, G, BT], f16)
        S1 = sb("S1", [P, BB, S])
        S2 = sb("S2", [P, BB, S])
        PR = sb("PR", [P, BB, S])
        mask = sb("mask", [P, S])
        ident = sb("ident", [P, P])
        ident16 = sb("ident16", [P, P], f16)
        smax = sb("smax", [P, BB])
        ssum = sb("ssum", [P, BB])
        srec = sb("srec", [P, BB])
        M = sb("M", [P, NC, E])
        LA = sb("LA", [P, NC, NLAB, R])
        LB = sb("LB", [P, E])
        bias = sb("bias", [P, E])
        onehot = sb("onehot", [P, TILES, NLAB])
        xtab = sb("xtab", [P, 4, TILES])
        unscale = sb("unscale", [P, 2, TILES])
        fsum = sb("fsum", [P, 16])
        wts = [sb(f"wts{p}", [P, WT]) for p in range(2)]
        label = sb("label", [P, TILES, TB], i32)
        cidx = sb("cidx", [P, 1], i32)
        xmaxs = sb("xmaxs", [P, 10])
        wmaxs = sb("wmaxs", [P, WT // 2])
        bounds = sb("bounds", [P, 8])
        wsc = [sb(f"wsc{p}", [P, 12]) for p in range(2)]
        fsc = sb("fsc", [P, 2])

        chf = CH[:, :, :].rearrange("p c t -> p (c t)").bitcast(f32)
        wbase_n = chf[:, 0:NC * E].rearrange("p (c e) -> p c e", c=NC)
        wffn_f = chf[:, NC * E:2 * NC * E].rearrange("p (c e) -> p c e", c=NC)
        wffn_t = chf[:, 2 * NC * E:3 * NC * E].rearrange("p (c e) -> p c e", c=NC)
        wffn_q = chf[:, 3 * NC * E:4 * NC * E].bitcast(i32).rearrange("p (c e) -> p c e", c=NC)
        clf = CL[:, :, :].rearrange("p c t -> p (c t)").bitcast(f32)
        lorab_n = clf[:, 0:NC * R].rearrange("p (c r) -> p c r", c=NC)
        lorab_4 = clf[:, 512:512 + NC * P].rearrange("p (c j r) -> p c j r", c=NC, j=4)
        wcond_n = clf[:, 256:384]
        gath = clf[:, 2048:2048 + S * S]
        wn1 = WN[1][:, :, :].rearrange("p r e -> p (r e)")
        bd = wn1[:, 0:TILES * P].rearrange("p (n t) -> p n t", n=TILES)
        at = [0]

        def last(*shape, dt=f32):
            n = 1
            for k in shape:
                n *= k
            words = n // 2 if dt == f16 else n
            ap = clf[:, at[0]:at[0] + words]
            at[0] += words
            ap = ap.bitcast(f16) if dt == f16 else ap
            if len(shape) == 3:
                ap = ap.rearrange("p (h c e) -> p h c e", h=shape[0], c=shape[1])
            return ap.rearrange("p (c e) -> p c e", c=shape[0]) if len(shape) == 2 else ap

        MHL = last(2, NC, E, dt=f16)
        LAHL = last(2, NC, NLAB * R, dt=f16)
        BST = last(E, dt=f16)
        XS = [last(E) for _ in range(2)]
        XTHL = [last(2, NC, P, dt=f16) for _ in range(2)]
        XB = [last(E) for _ in range(2)]
        OT = [last(E) for _ in range(2)]
        LOWM = last(NLAB, R)
        LOWF = [last(R) for _ in range(2)]
        LOWS = [last(4, R, dt=f16) for _ in range(2)]
        LOWT = [last(P, dt=f16) for _ in range(2)]
        assert at[0] <= NC * TOK // 2

        pQ = [pb(f"pQ{n}", [P, 512]) for n in range(2)]
        pKV = pb("pKV", [P, 512])
        pS = pb("pS", [P, 512])
        pT = pb("pT", [P, 512])
        pA = [pb(f"pA{n}", [P, 512]) for n in range(2)]
        pD = pb("pD", [P, 512])
        pC = [*pQ, pS, pT]
        pT16 = pT[:, :].bitcast(f16)

        names = """ffnw_in small_in la_in cond_in gath_in gath_out bd_in wn_in v_stacked
            pool_turn dense_zeroed chain ffn_ready ffn_t ffn_tc m_done m_copied
            xmax_ready bounds_ready cscale_ready c_done c_hi c_lo onehot_ready
            stage_full w_t w_hi w_lo wscale_ready escale_ready wmax_part wmax_ready wmax_all xmax_all
            k_done q_done v_done s_done t_done a_done d_done
            k_hi k_lo q_hi q_lo v_hi v_lo pt_copied a_hi a_lo s_read s_sub exp_done p_full p_hi p_lo x2_done
            x2_max x2_scaled f_max f_all lb4_ready f_scaled m_hi m_lo xs_ready xb_ready xt_t xt_hi xt_lo y_done
            low_done low_full low_hi low_lo low_t lowt_copied yb_done yb_read ot_ready""".split()
        s = {n: sem(n) for n in names}
        XPARTS = 8
        x_in = [sem(f"x_in{n}") for n in range(XPARTS)]
        out_done = [sem(f"out_done{m}") for m in range(2)]
        FREE, FREE_DMA = 1, 16

        def half_of(par, r, h):
            if isinstance(r, int):
                return WH[par][:, r, h, :, :]
            return WH[par][:, bass.ds(r, 1), h, :, :].rearrange("p o c d -> p (o c) d")

        def two_heads(q, n):
            return q[:, :, 2 * n:2 * n + 2, :].rearrange("p b g t -> p b (g t)")

        def tile_of(x, n):
            return x[:, bass.ds(n, 1), :].rearrange("p o e -> p (o e)")

        def chunks(ap):
            return ap.rearrange("p (c d) -> p c d", c=NC)

        block = ctx.enter_context(nc.Block())

        def steps(eng, first, rest):
            with eng.Fori(0, KV // 2) as pair:
                for par in range(2):
                    base = pair * (2 * BLOCKS) + par * BLOCKS
                    first(base, par, pair)
                    with eng.Fori(1, PREP_AT) as blk:
                        rest(base + blk, par, blk, None)
                    with eng.Fori(PREP_AT, BLOCKS) as blk:
                        rest(base + blk, par, blk, ((pair * (2 * WT) + (par + 1) * WT) + (blk - PREP_AT),
                                                    pair * 2 + (par + 2)))

        def tail(eng, ahead, before, here, after, last=None):
            def call(f, n, m):
                if f is not None:
                    f(n, m)

            call(ahead, 0, 0)
            call(ahead, 1, 1)
            call(here, 0, 0)
            call(last, 0, 0)
            with eng.Fori(0, TILES // 2 - 1) as pair:
                for k in range(2):
                    n = pair * 2 + (k + 1)
                    call(ahead, n + 1, k)
                    call(before, n - 1, k)
                    call(here, n, 1 - k)
                    call(after, n - 1, k)
                    call(last, n, 1 - k)
            call(before, TILES - 2, 0)
            call(here, TILES - 1, 1)
            call(after, TILES - 2, 0)
            call(last, TILES - 1, 1)
            call(before, TILES - 1, 1)
            call(after, TILES - 1, 1)

        @block.sync
        def _(sp):
            sp.nop().then_inc(s["v_stacked"], FREE_DMA)
            for m in range(2):
                sp.nop().then_inc(out_done[m], FREE_DMA)
            sp.dma_start(wffn_q, q_ffn.rearrange("(c p) e -> p c e", p=P)).then_inc(s["ffnw_in"], 16)
            sp.dma_start(wbase_n, w_base.rearrange("(c p) e -> p c e", p=P)).then_inc(s["ffnw_in"], 16)
            sp.dma_start(lorab_n, lora_b.rearrange("(c p) r -> p c r", p=P)).then_inc(s["ffnw_in"], 16)

            def load_weights(par, kv):
                q = w_qkv[bass.ds(kv * (G * D), G * D), :] if not isinstance(kv, int) else w_qkv[kv * G * D:(kv + 1) * G * D, :]
                k = w_qkv[bass.ds(kv * D + HEADS * D, D), :]
                v = w_qkv[bass.ds(kv * D + (HEADS + KV) * D, D), :]
                d = w_dense[:, bass.ds(kv * (G * D), G * D)]
                sp.dma_start(WN[par][:, 0:G, :], q.rearrange("(g p) e -> p g e", p=P)).then_inc(s["wn_in"], 16)
                sp.dma_start(WN[par][:, KT, :], k).then_inc(s["wn_in"], 16)
                sp.dma_start(WN[par][:, VT, :], v).then_inc(s["wn_in"], 16)
                sp.dma_start(WN[par][:, DT:WT, :], d.rearrange("(c p) e -> p c e", p=P)).then_inc(s["wn_in"], 16)

            load_weights(0, 0)
            for n in range(XPARTS):
                part = slice(n * TILES // XPARTS, (n + 1) * TILES // XPARTS)
                sp.dma_start(X2[:, part, :], x_t[:, part, :]).then_inc(x_in[n], 16)
                if n == 2:
                    sp.wait_ge(s["gath_in"], 16)
                    sp.dma_start(gathered, gath).then_inc(s["gath_out"], 16)
                if n == 4:
                    sp.wait_ge(s["gath_out"], 16)
                    sp.wait_ge(s["pool_turn"], IDENTS_TURN + 1)
                    src = gathered.rearrange("(n a) (c d) -> a c n d", a=TB, c=S)
                    for a in range(TB):
                        sp.dma_start(bd[a * S:(a + 1) * S, :, a * S:(a + 1) * S], src[a]).then_inc(s["bd_in"], 16)

            def stack_values(i):
                sp.wait_ge(s["v_lo"], i + 1 + FREE)
                sp.wait_ge(s["a_done"], i * 2 + 2)
                for a in range(TB):
                    for j in range(4):
                        sp.dma_start(VST[j * S:(j + 1) * S, a::TB, :],
                                     VHL[a * S:(a + 1) * S, :, j // 2, :]).then_inc(s["v_stacked"], 16)

            def first(i, par, pair):
                stack_values(i)
                sp.wait_ge(s["x2_done"], i * 2 + 2 + FREE)
                if par == 0:
                    sp.wait_ge(s["c_lo"], TILES)
                load_weights(1 - par, pair * 2 + 1 if par == 0 else (pair * 2 + 2) % KV)

            def rest(i, par, blk, prep):
                stack_values(i)

            steps(sp, first, rest)
            with sp.Fori(0, TILES // 2) as pair:
                for n in range(2):
                    sp.wait_ge(s["ot_ready"], pair * 2 + n + 1 + FREE)
                    sp.dma_start(out_t[pair * 2 + n, :, :], OT[n]).then_inc(out_done[n], 16)
            for m in range(2):
                sp.wait_ge(out_done[m], 16 * TILES // 2 + FREE_DMA)

        @block.gpsimd
        def _(pool):
            pool.dma_start(cidx[:, :], cond_index.rearrange("(b o) -> b o", o=1)).then_inc(s["cond_in"], 16)
            turns = [0]

            def turn(ins):
                turns[0] += 1
                ins.then_inc(s["pool_turn"], 1)
                pool.wait_ge(s["pool_turn"], turns[0])

            turn(pool.memset(ident[:, :], 0.0))
            turn(pool.affine_select(out=ident[:, :], in_=ident[:, :], compare_op=ALU.not_equal, fill=1.0, base=0,
                                    pattern=[[-1, P]], channel_multiplier=1))
            turn(pool.tensor_copy(ident16[:, :], ident[:, :]))
            assert turns[0] == IDENTS_TURN
            turn(pool.memset(wn1, 0.0))
            pool.wait_ge(s["cond_in"], 16)
            pool.indirect_dma_start(gath, None, w_cond.rearrange("n c d -> n (c d)"),
                                    bass.IndirectOffsetOnAxis(ap=cidx[:, 0:1], axis=0)).then_inc(s["gath_in"], 16)
            pool.wait_ge(s["gath_in"], 16)
            turn(pool.memset(mask[:, :], 0.0))
            for q in range(4):
                m = mask[q * S:(q + 1) * S, :]
                turn(pool.affine_select(out=m, in_=m, compare_op=ALU.is_ge, fill=1.0, base=0,
                                        pattern=[[-1, S]], channel_multiplier=1))
            turn(pool.tensor_scalar(mask[:, :], mask[:, :], MASKED, None, ALU.mult))
            turn(pool.memset(PST[:, :, :, :], 0.0))
            turn(pool.memset(VST[:, :, :], 0.0))
            turn(pool.memset(wsc[1][:, :], 0.0))
            assert turns[0] == POOL_TURNS

            def stage_tile(par, r, n):
                pool.wait_ge(s["w_t"], n)
                src = WN[par][:, bass.ds(r, 1), :].rearrange("p o e -> p (o e)")
                pool.tensor_copy(ST[:, :], src).then_inc(s["stage_full"], 1)

            pool.wait_ge(s["wmax_ready"], 2)
            pool.partition_all_reduce(wsc[0][:, 0:2], wsc[0][:, 6:8], P, RED.absmax).then_inc(s["wmax_all"], 1)
            pool.wait_ge(s["wmax_all"], 1)
            pool.wait_ge(s["xmax_ready"], 1)
            pool.partition_all_reduce(bounds[:, 0:2], xmaxs[:, 8:10], P, RED.absmax).then_inc(s["xmax_all"], 1)
            pool.wait_ge(s["xmax_all"], 1)
            pool.wait_ge(s["c_done"], TILES)
            pool.memset(wn1[:, DT * E:TILES * P], 0.0).then_inc(s["dense_zeroed"], 1)
            pool.wait_ge(s["dense_zeroed"], 1)
            pool.wait_ge(s["f_max"], 3)
            pool.partition_all_reduce(fsum[:, 3:6], fsum[:, 0:3], P, RED.absmax).then_inc(s["f_all"], 1)
            pool.wait_ge(s["f_all"], 1)

            for kv in range(KV):
                sc = wsc[(kv + 1) % 2]
                pool.wait_ge(s["wmax_ready"], 2 * (kv + 2))
                pool.partition_all_reduce(sc[:, 0:2], sc[:, 6:8], P, RED.absmax).then_inc(s["wmax_all"], 1)
                pool.wait_ge(s["wmax_all"], kv + 2)
                with pool.Fori(0, WT) as r:
                    stage_tile((kv + 1) % 2, r, (kv + 1) * WT + r)

            pool.wait_ge(s["x2_done"], 2 * (KV * BLOCKS + 1) + FREE)
            for n in range(2):
                pool.tensor_tensor(XB[n], X2[:, n, :], bias[:, :], ALU.add).then_inc(s["xb_ready"], 1)
            with pool.Fori(1, TILES // 2) as pair:
                for m in range(2):
                    n = pair * 2 + m
                    pool.wait_ge(s["ot_ready"], n - 1 + FREE)
                    pool.tensor_tensor(XB[m], tile_of(X2, n), bias[:, :], ALU.add).then_inc(s["xb_ready"], 1)

        @block.scalar
        def _(act):
            act.dma_start(wcond_n, w_cond.rearrange("n c d -> (n c d)").rearrange("(p f) -> p f", p=P)).then_inc(s["small_in"], 16)
            act.dma_start(fsc[:, 0:1], ffn_scale.rearrange("(o n) -> o n", o=1).to_broadcast([P, 1])).then_inc(s["small_in"], 16)
            act.dma_start(fsc[:, 1:2], ffn_zero.rearrange("(o n) -> o n", o=1).to_broadcast([P, 1])).then_inc(s["small_in"], 16)
            act.dma_start(label[:, :, :].rearrange("p n a -> p (n a)"),
                          label_index.rearrange("(o b) -> o b", o=1).to_broadcast([P, B])).then_inc(s["small_in"], 16)
            for c in range(NC):
                act.dma_start(LA[:, c, :, :], lora_a[:, c * P:(c + 1) * P, :].rearrange("l p r -> p l r")).then_inc(s["la_in"], 16)
            act.dma_start(bias[:, :], ffn_bias.rearrange("(o n) -> o n", o=1).to_broadcast([P, E])).then_inc(s["la_in"], 16)

            for c in range(NC):
                act.wait_ge(s["ffn_t"], c + 1)
                act.activation(wffn_t[:, :, c * P:(c + 1) * P], chunks(pQ[c % 2][:, :]), ACT.Copy).then_inc(s["ffn_tc"], 1)
            def weight_hi(par, r, n):
                act.wait_ge(s["w_t"], n + 1)
                act.activation(half_of(par, r, 0), chunks(pKV[:, :]), ACT.Copy,
                               scale=wts[par][:, bass.ds(r, 1)]).then_inc(s["w_hi"], 1)

            act.wait_ge(s["wscale_ready"], 1)
            for r in range(WT):
                act.wait_ge(s["w_t"], r + 1)
                act.activation(half_of(0, r, 0), chunks(pA[r % 2][:, :]), ACT.Copy,
                               scale=wts[0][:, r:r + 1]).then_inc(s["w_hi"], 1)
            for c in range(NC):
                act.wait_ge(s["m_done"], c + 1)
                act.activation(M[:, c, :], pA[c % 2][:, :], ACT.Copy).then_inc(s["m_copied"], 1)
            act.wait_ge(s["m_done"], NC + 1)
            act.activation(LB[:, :], pD[:, :], ACT.Copy, scale=0.5).then_inc(s["m_copied"], 1)
            act.wait_ge(s["cscale_ready"], 1)
            with act.Fori(0, TILES // 4) as four:
                for m in range(4):
                    n = four * 4 + m
                    act.wait_ge(s["c_done"], n + 1)
                    act.activation(CH[:, :, bass.ds(n * P, P)], chunks(pC[m][:, :]), ACT.Copy,
                                   scale=bounds[:, 6:7]).then_inc(s["c_hi"], 1)

            def values(i):
                act.wait_ge(s["v_done"], i + 1)
                act.wait_ge(s["v_stacked"], i * (16 * VDMAS) + FREE_DMA)
                act.activation(VHL[:, :, 0, :], pKV[:, 0:BTILES * D].rearrange("p (n d) -> p n d", n=BTILES),
                               ACT.Copy, scale=EVAC).then_inc(s["v_hi"], 1)

            def keys(i):
                act.wait_ge(s["k_done"], i + 1)
                act.activation(KHL[:, :, 0, :], pD[:, 0:BT].rearrange("p (b t) -> p b t", b=BB), ACT.Copy,
                               scale=EVAC).then_inc(s["k_hi"], 1)

            def queries(i, n):
                act.wait_ge(s["q_done"], i * 2 + (n + 1))
                act.activation(two_heads(QH, n), pQ[n][:, :].rearrange("p (b n) -> p b n", b=BB),
                               ACT.Copy, scale=EVAC).then_inc(s["q_hi"], 1)

            def attend(i):
                act.wait_ge(s["t_done"], i + 1)
                act.activation(PT[:, :, :], pT16[:, :].rearrange("p (b t) -> p b t", b=BB), ACT.Copy
                               ).then_inc(s["pt_copied"], 1)

            def attended(i):
                for n in range(2):
                    act.wait_ge(s["a_done"], i * 2 + (n + 1))
                    act.activation(AH[:, :, n * P:(n + 1) * P], pA[n][:, :].rearrange("p (g n) -> p g n", g=G),
                                   ACT.Copy).then_inc(s["a_hi"], 1)

            def softmax(i, par):
                act.wait_ge(s["s_sub"], i + 1)
                act.activation(S2[:, :, :], S1[:, :, :], ACT.Exp, scale=wsc[par][:, 9:10]).then_inc(s["exp_done"], 1)
                act.wait_ge(s["p_full"], i + 1)
                act.activation(PST[:, :, 0::2, :], PR[:, :, :].unsqueeze(2).to_broadcast([P, BB, 2, S]),
                               ACT.Copy).then_inc(s["p_hi"], 1)

            def step(i, par, blk, prep):
                values(i)
                keys(i)
                queries(i, 0)
                attend(i)
                attended(i)
                queries(i, 1)
                if prep is not None:
                    act.wait_ge(s["wscale_ready"], prep[1])
                    weight_hi(1 - par, blk - PREP_AT, prep[0])
                softmax(i, par)

            act.wait_ge(s["pool_turn"], POOL_TURNS)
            steps(act, lambda i, par, pair: step(i, par, 0, None), step)
            attend(KV * BLOCKS)
            attended(KV * BLOCKS)

            act.wait_ge(s["f_scaled"], 1)
            act.activation(MHL[:, 0, :, :], M[:, :, :], ACT.Copy, scale=fsum[:, 12:13]).then_inc(s["m_hi"], 1)
            act.activation(LAHL[:, 0, :, :], LA[:, :, :, :].rearrange("p c l r -> p c (l r)"), ACT.Copy,
                           scale=fsum[:, 13:14]).then_inc(s["m_hi"], 1)
            act.activation(BST, LB[:, :], ACT.Copy, scale=fsum[:, 14:15]).then_inc(s["m_hi"], 1)

            def scaled(n, m):
                act.wait_ge(s["x2_scaled"], 1)
                act.activation(XS[m], tile_of(X2, n), ACT.Copy, scale=xtab[:, 3, bass.ds(n, 1)]).then_inc(s["xs_ready"], 1)
                act.wait_ge(s["xt_t"], n + 1)
                act.activation(XTHL[m][:, 0, :, :], chunks(pQ[m][:, :]), ACT.Copy).then_inc(s["xt_hi"], 1)

            def low_rank(n, m):
                act.wait_ge(s["low_full"], n + 1)
                act.activation(LOWS[m][:, 0::2, :], LOWF[m].unsqueeze(1).to_broadcast([P, 2, R]),
                               ACT.Copy).then_inc(s["low_hi"], 1)

            def low_rank_t(n, m):
                act.wait_ge(s["low_t"], n + 1)
                act.activation(LOWT[m], pT16[:, 0:P], ACT.Copy).then_inc(s["lowt_copied"], 1)

            tail(act, lambda n, m: scaled(n, m), low_rank_t, low_rank, None)

        @block.vector
        def _(dve):
            def chained(instructions, base):
                n = 0
                for ins in instructions:
                    n += 1
                    ins.then_inc(s["chain"], 1)
                    dve.wait_ge(s["chain"], base + n)
                return n

            def powers(src, power, inverse):
                yield dve.tensor_scalar(power, src, 1e-30, 2.0, ALU.max, ALU.mult)
                yield dve.tensor_scalar(power.bitcast(i32), power.bitcast(i32), 0x7F800000, None, ALU.bitwise_and)
                yield dve.tensor_scalar(inverse.bitcast(i32), power.bitcast(i32), -1.0, float(254 << 23),
                                        ALU.mult, ALU.add)

            def max_pair(par, k):
                src = WN[par][:, bass.ds(k * 2, 2), :].rearrange("p r e -> p (r e)")
                dve.tensor_reduce(wmaxs[:, bass.ds(k, 1)], src, AX.X, ALU.max, apply_absolute_value=True
                                  ).then_inc(s["wmax_part"], 1)

            def head_max(par, n):
                dve.wait_ge(s["wmax_part"], n)
                dve.tensor_reduce(wsc[par][:, 6:7], wmaxs[:, 0:DT // 2], AX.X, ALU.max).then_inc(s["wmax_ready"], 1)
                dve.tensor_reduce(wsc[par][:, 7:8], wmaxs[:, DT // 2:WT // 2], AX.X, ALU.max).then_inc(s["wmax_ready"], 1)

            def tile_scales(par):
                sc = wsc[par]
                yield from powers(sc[:, 0:2], sc[:, 2:4], sc[:, 4:6])
                for k, (lo, hi) in enumerate(((0, DT), (DT, WT))):
                    ins = dve.tensor_scalar(wts[par][:, lo:hi], sc[:, 4 + k:5 + k].to_broadcast([P, hi - lo]),
                                            SPLIT, None, ALU.mult)
                    yield ins

            def stage_scales(par):
                sc = wsc[par]
                yield dve.tensor_scalar(sc[:, 8:9], sc[:, 2:3], bounds[:, 4:5], E / SPLIT, ALU.mult, ALU.mult)
                yield dve.scalar_tensor_tensor(sc[:, 9:10], sc[:, 8:9], float(D) ** -0.5, sc[:, 8:9],
                                               ALU.mult, ALU.mult)
                yield dve.tensor_scalar(sc[:, 10:11], sc[:, 3:4], sc[:, 8:9], 1.0 / SPLIT, ALU.mult, ALU.mult)

            for name in "v_lo q_lo p_lo x2_done a_lo s_read w_lo yb_read ot_ready".split():
                dve.nop().then_inc(s[name], FREE)
            dve.wait_ge(s["ffnw_in"], 48)
            dve.wait_ge(s["small_in"], 64)
            dve.tensor_scalar(wffn_f, wffn_q, fsc[:, 1:2], fsc[:, 0:1], ALU.subtract, ALU.mult).then_inc(s["ffn_ready"], 1)
            dve.tensor_copy(lorab_4, lorab_n.unsqueeze(2).to_broadcast([P, NC, 4, R])).then_inc(s["lb4_ready"], 1)
            dve.tensor_reduce(xmaxs[:, 9:10], wcond_n, AX.X, ALU.max, apply_absolute_value=True).then_inc(s["chain"], 1)
            for l in range(NLAB):
                for a in range(TB):
                    dve.tensor_scalar(onehot[a * S:(a + 1) * S, :, l], label[a * S:(a + 1) * S, :, a], float(l), EVAC,
                                      ALU.is_equal, ALU.mult).then_inc(s["onehot_ready"], 1)

            def weight_lo(par, r, n):
                dve.wait_ge(s["w_hi"], n + 1)
                dve.scalar_tensor_tensor(half_of(par, r, 1), chunks(pKV[:, :]), wts[par][:, bass.ds(r, 1)],
                                         half_of(par, r, 0), ALU.mult, ALU.subtract).then_inc(s["w_lo"], 1)

            dve.wait_ge(s["wn_in"], 64)
            for k in range(WT // 2):
                max_pair(0, k)
            head_max(0, WT // 2)
            dve.wait_ge(s["wmax_all"], 1)
            n_tiles = chained(tile_scales(0), 1)
            dve.tensor_copy(wsc[0][:, 11:12], wts[0][:, 0:1]).then_inc(s["wscale_ready"], 1)
            def x_max(n):
                dve.wait_ge(x_in[n], 16)
                part = slice(n * TILES // XPARTS, (n + 1) * TILES // XPARTS)
                dve.tensor_reduce(xmaxs[:, n:n + 1], X2[:, part, :].rearrange("p n e -> p (n e)"),
                                  AX.X, ALU.max, apply_absolute_value=True).then_inc(s["chain"], 1)

            for r in range(WT):
                dve.wait_ge(s["w_hi"], r + 1)
                dve.scalar_tensor_tensor(half_of(0, r, 1), chunks(pA[r % 2][:, :]), wts[0][:, r:r + 1],
                                         half_of(0, r, 0), ALU.mult, ALU.subtract).then_inc(s["w_lo"], 1)
                if r % 2:
                    x_max(r // 2)
            for n in range(WT // 2, XPARTS):
                x_max(n)
            dve.wait_ge(s["chain"], n_tiles + 9)
            dve.tensor_reduce(xmaxs[:, 8:9], xmaxs[:, 0:8], AX.X, ALU.max).then_inc(s["xmax_ready"], 1)

            def c_scale():
                yield from powers(bounds[:, 0:2], bounds[:, 2:4], xmaxs[:, 0:2])
                yield dve.tensor_scalar(bounds[:, 4:5], bounds[:, 2:3], bounds[:, 3:4], float(S), ALU.mult, ALU.mult)
                yield dve.tensor_scalar(bounds[:, 5:6].bitcast(i32), bounds[:, 4:5].bitcast(i32), -1.0,
                                        float(254 << 23), ALU.mult, ALU.add)

            dve.wait_ge(s["xmax_all"], 1)
            n_c = chained(c_scale(), n_tiles + 9)
            dve.tensor_scalar(bounds[:, 6:7], bounds[:, 5:6], SPLIT, None, ALU.mult).then_inc(s["cscale_ready"], 1)
            n_stage = chained(stage_scales(0), n_tiles + 9 + n_c)
            dve.wait_ge(s["cscale_ready"], 1)
            used, per_head = n_tiles + 9 + n_c + n_stage, n_tiles + n_stage
            with dve.Fori(0, TILES // 4) as four:
                for m in range(4):
                    n = four * 4 + m
                    dve.wait_ge(s["c_hi"], n + 1)
                    dve.scalar_tensor_tensor(CL[:, :, bass.ds(n * P, P)], chunks(pC[m][:, :]), bounds[:, 6:7],
                                             CH[:, :, bass.ds(n * P, P)], ALU.mult, ALU.subtract).then_inc(s["c_lo"], 1)

            dve.wait_ge(s["la_in"], 16 * (NC + 1))
            dve.wait_ge(s["m_copied"], NC + 1)
            for n, part in enumerate((M[:, :, :].rearrange("p c e -> p (c e)"),
                                      LA[:, :, :, :].rearrange("p c l r -> p (c l r)"), LB[:, :])):
                dve.tensor_reduce(fsum[:, n:n + 1], part, AX.X, ALU.max, apply_absolute_value=True
                                  ).then_inc(s["f_max"], 1)

            def low(out, psum, high, done, scale=EVAC):
                dve.scalar_tensor_tensor(out, psum, scale, high, ALU.mult, ALU.subtract).then_inc(s[done], 1)

            def values(i):
                dve.wait_ge(s["v_hi"], i + 1)
                low(VHL[:, :, 1, :], pKV[:, 0:BTILES * D].rearrange("p (n d) -> p n d", n=BTILES),
                    VHL[:, :, 0, :], "v_lo")

            def keys(i):
                dve.wait_ge(s["k_hi"], i + 1)
                low(KHL[:, :, 1, :], pD[:, 0:BT].rearrange("p (b t) -> p b t", b=BB), KHL[:, :, 0, :], "k_lo")

            def queries(i, n):
                dve.wait_ge(s["q_hi"], i * 2 + (n + 1))
                low(two_heads(QL, n), pQ[n][:, :].rearrange("p (b n) -> p b n", b=BB), two_heads(QH, n), "q_lo")

            def attended(i):
                for n in range(2):
                    dve.wait_ge(s["a_hi"], i * 2 + (n + 1))
                    low(AL[:, :, n * P:(n + 1) * P], pA[n][:, :].rearrange("p (g n) -> p g n", g=G),
                        AH[:, :, n * P:(n + 1) * P], "a_lo", 1.0)

            def spread(row):
                return row.unsqueeze(2).to_broadcast([P, BB, S])

            def scores(i, base):
                dve.wait_ge(s["s_done"], i + 1)
                sc = pS[:, :].rearrange("p (b h t) -> p b h t", b=BB, h=2)
                chained([dve.tensor_tensor(S1[:, :, :], sc[:, :, 0, :],
                                           mask[:, :].unsqueeze(1).to_broadcast([P, BB, S]), ALU.add)], base)
                dve.tensor_tensor(S2[:, :, :], S1[:, :, :], sc[:, :, 1, :], ALU.add).then_inc(s["s_read"], 1)
                dve.wait_ge(s["s_read"], i + 1 + FREE)
                chained([dve.tensor_reduce(smax[:, :], S2[:, :, :], AX.X, ALU.max)], base + 1)
                dve.tensor_tensor(S1[:, :, :], S2[:, :, :], spread(smax[:, :]), ALU.subtract).then_inc(s["s_sub"], 1)

            def probabilities(i, base):
                dve.wait_ge(s["exp_done"], i + 1)
                chained([dve.tensor_reduce(ssum[:, :], S2[:, :, :], AX.X, ALU.add)], base)
                chained([dve.reciprocal(srec[:, :], ssum[:, :])], base + 1)
                dve.tensor_tensor(PR[:, :, :], S2[:, :, :], spread(srec[:, :]), ALU.mult).then_inc(s["p_full"], 1)
                dve.wait_ge(s["p_hi"], i + 1)
                dve.tensor_tensor(PST[:, :, 1::2, :], PR[:, :, :].unsqueeze(2).to_broadcast([P, BB, 2, S]),
                                  PST[:, :, 0::2, :], ALU.subtract).then_inc(s["p_lo"], 1)

            def update(i, par, tile, n):
                dve.wait_ge(s["d_done"], i * 2 + (n + 1))
                t = X2[:, bass.ds(tile, 1), :].rearrange("p o e -> p (o e)")
                dve.scalar_tensor_tensor(t, [pD, pT][n][:, :], wsc[par][:, 10:11], t, ALU.mult, ALU.add
                                         ).then_inc(s["x2_done"], 1)
                if par == 1:
                    dve.wait_ge(s["x2_done"], i * 2 + (n + 1) + FREE)
                    dve.tensor_reduce(xtab[:, 0, bass.ds(tile, 1)], t, AX.X, ALU.max, apply_absolute_value=True
                                      ).then_inc(s["x2_max"], 1)

            PER = 4

            def step(i, par, before, blk, prep, tile, head, loads=None):
                base = i * PER + head + used
                values(i)
                keys(i)
                queries(i, 0)
                attended(i)
                queries(i, 1)
                if prep is not None:
                    weight_lo(1 - par, blk - PREP_AT, prep)
                update(i, before, tile, 0)
                scores(i, base)
                update(i, before, tile + 1, 1)
                probabilities(i, base + 2)
                if prep is None and not isinstance(blk, int):
                    dve.wait_ge(s["wn_in"], loads)
                    max_pair(1 - par, blk - 1)

            last_tile = (BLOCKS - 1) * BTILES
            dve.wait_ge(s["pool_turn"], POOL_TURNS)
            with dve.Fori(0, KV // 2) as pair:
                for par in range(2):
                    start = pair * (2 * BLOCKS) + par * BLOCKS
                    prep = pair * (2 * WT) + (par + 1) * WT
                    head = pair * (2 * per_head) + par * per_head
                    step(start, par, 1 - par, 0, None, last_tile, head)
                    with dve.Fori(1, PREP_AT) as blk:
                        step(start + blk, par, par, blk, None, (blk - 1) * BTILES, head, pair * 128 + (par + 2) * 64)
                    head_max(1 - par, (pair * WT + (par + 2) * (WT // 2)))
                    dve.wait_ge(s["wmax_all"], pair * 2 + (par + 2))
                    base = (start + PREP_AT) * PER + head + used
                    chained(tile_scales(1 - par), base)
                    chained(stage_scales(1 - par), base + n_tiles)
                    dve.tensor_copy(wsc[1 - par][:, 11:12], wts[1 - par][:, 0:1]).then_inc(s["wscale_ready"], 1)
                    with dve.Fori(PREP_AT, BLOCKS) as blk:
                        step(start + blk, par, par, blk, prep + (blk - PREP_AT), (blk - 1) * BTILES, head + per_head)
            attended(KV * BLOCKS)
            for n in range(2):
                update(KV * BLOCKS, 1, last_tile + n, n)

            dve.wait_ge(s["x2_max"], KV * BLOCKS + 2)
            dve.wait_ge(s["f_all"], 1)

            def last_scales():
                yield from powers(xtab[:, 0, :], xtab[:, 1, :], xtab[:, 2, :])
                yield dve.tensor_scalar(xtab[:, 3, :], xtab[:, 2, :], SPLIT, None, ALU.mult)
                yield from powers(fsum[:, 3:6], fsum[:, 6:9], fsum[:, 9:12])
                yield dve.tensor_scalar(fsum[:, 12:15], fsum[:, 9:12], SPLIT, None, ALU.mult)
                yield dve.tensor_tensor(fsum[:, 15:16], fsum[:, 7:8], fsum[:, 8:9], ALU.mult)
                yield dve.tensor_scalar(unscale[:, 0, :], xtab[:, 1, :], fsum[:, 6:7], SPLIT ** -2, ALU.mult, ALU.mult)
                yield dve.tensor_scalar(unscale[:, 1, :], xtab[:, 1, :], fsum[:, 15:16], SPLIT ** -3 / EVAC,
                                        ALU.mult, ALU.mult)

            done = KV * BLOCKS * PER + used + KV * per_head
            done += chained(last_scales(), done)
            dve.wait_ge(s["q_done"], 2 * KV * BLOCKS)
            dve.nop().then_inc(s["f_scaled"], 1)
            dve.nop().then_inc(s["x2_scaled"], 1)
            dve.wait_ge(s["m_hi"], 1)
            dve.scalar_tensor_tensor(MHL[:, 1, :, :], M[:, :, :], fsum[:, 12:13], MHL[:, 0, :, :],
                                     ALU.mult, ALU.subtract).then_inc(s["m_lo"], 1)
            dve.wait_ge(s["m_hi"], 3)
            dve.scalar_tensor_tensor(LAHL[:, 1, :, :], LA[:, :, :, :].rearrange("p c l r -> p c (l r)"), fsum[:, 13:14],
                                     LAHL[:, 0, :, :], ALU.mult, ALU.subtract).then_inc(s["m_lo"], 1)
            half_p = slice(P // 2, P)
            dve.scalar_tensor_tensor(BST[half_p, :], LB[half_p, :], fsum[half_p, 14:15], BST[half_p, :],
                                     ALU.mult, ALU.subtract).then_inc(s["m_lo"], 1)

            def scaled(n, m):
                dve.wait_ge(s["xt_hi"], n + 1)
                dve.tensor_tensor(XTHL[m][:, 1, :, :], chunks(pQ[m][:, :]), XTHL[m][:, 0, :, :],
                                  ALU.subtract).then_inc(s["xt_lo"], 1)

            def low_rank(n, m):
                dve.wait_ge(s["low_done"], n + 1)
                which = onehot[:, bass.ds(n, 1), :].rearrange("p o l -> p (o l)").unsqueeze(2).to_broadcast([P, NLAB, R])
                chained([dve.tensor_tensor(LOWM, (pS, pKV)[m][:, 0:NLAB * R].rearrange("p (l r) -> p l r", l=NLAB),
                                           which, ALU.mult)], n + done)
                dve.tensor_reduce(LOWF[m], LOWM.rearrange("p l r -> p r l"), AX.X, ALU.add).then_inc(s["low_full"], 1)
                dve.wait_ge(s["low_hi"], n + 1)
                dve.tensor_tensor(LOWS[m][:, 1::2, :], LOWF[m].unsqueeze(1).to_broadcast([P, 2, R]),
                                  LOWS[m][:, 0::2, :], ALU.subtract).then_inc(s["low_lo"], 1)

            def output(n, m):
                dve.wait_ge(s["yb_done"], n + 1)
                dve.wait_ge(s["xb_ready"], n + 1)
                dve.wait_ge(out_done[m], (n - m) * 8 + FREE_DMA)
                dve.scalar_tensor_tensor(OT[m], pD[:, :], unscale[:, 1, bass.ds(n, 1)], XB[m], ALU.mult, ALU.add
                                         ).then_inc(s["yb_read"], 1)
                dve.wait_ge(s["yb_read"], n + 1 + FREE)
                dve.wait_ge(s["y_done"], n + 1)
                dve.scalar_tensor_tensor(OT[m], pA[m][:, :], unscale[:, 0, bass.ds(n, 1)], OT[m], ALU.mult, ALU.add
                                         ).then_inc(s["ot_ready"], 1)

            tail(dve, scaled, None, low_rank, output)

        @block.tensor
        def _(pe):
            mm = nc.tensor.matmul
            pe.wait_ge(s["pool_turn"], IDENTS_TURN)
            pe.wait_ge(s["ffn_ready"], 1)
            for oc in range(NC):
                if oc >= 2:
                    pe.wait_ge(s["ffn_tc"], oc - 1)
                for mc in range(NC):
                    last = nc.tensor.transpose(pQ[oc % 2][:, mc * P:(mc + 1) * P],
                                               wffn_f[:, oc, mc * P:(mc + 1) * P], ident[:, :])
                last.then_inc(s["ffn_t"], 1)
            pe.wait_ge(s["wn_in"], 64)
            for r in range(WT):
                if r >= 2:
                    pe.wait_ge(s["w_lo"], r - 1 + FREE)
                for c in range(NC):
                    last_mm = nc.tensor.transpose(pA[r % 2][:, c * P:(c + 1) * P], WN[0][:, r, c * P:(c + 1) * P], ident[:, :])
                last_mm.then_inc(s["w_t"], 1)
            pe.wait_ge(s["w_lo"], WT + FREE)
            pe.wait_ge(s["ffn_tc"], NC)
            pe.wait_ge(s["lb4_ready"], 1)
            for ic in range(NC):
                if ic >= 2:
                    pe.wait_ge(s["m_copied"], ic - 1)
                for mc in range(NC):
                    last = mm(pA[ic % 2][:, :], wbase_n[:, mc, ic * P:(ic + 1) * P], wffn_t[:, mc, :],
                              start=(mc == 0), stop=(mc == NC - 1))
                last.then_inc(s["m_done"], 1)
            for mc in range(NC):
                last = mm(pD[:, :], lorab_4[:, mc, :, :].rearrange("p j r -> p (j r)"), wffn_t[:, mc, :],
                          start=(mc == 0), stop=(mc == NC - 1))
            last.then_inc(s["m_done"], 1)

            def weight_tile(n, i):
                pe.wait_ge(s["stage_full"], n - WT + 1)
                pe.wait_ge(s["v_lo"], i + 1 + FREE)
                for c in range(NC):
                    last = nc.tensor.transpose(pKV[:, c * P:(c + 1) * P], ST[:, c * P:(c + 1) * P], ident[:, :])
                last.then_inc(s["w_t"], 1)

            pe.wait_ge(s["bd_in"], 16 * TB)
            for n in range(XPARTS):
                pe.wait_ge(x_in[n], 16)
            for n in range(TILES):
                if n >= 4:
                    pe.wait_ge(s["c_lo"], n - 3)
                for c in range(NC):
                    last = mm(pC[n % 4][:, c * P:(c + 1) * P], X2[:, n, c * P:(c + 1) * P], bd[:, n, :],
                              start=True, stop=True)
                last.then_inc(s["c_done"], 1)
            pe.wait_ge(s["c_lo"], TILES)

            HL = ((0, 0), (0, 1), (1, 0))

            def half(h, c, lo, n):
                return (CH, CL)[h][:, c, bass.ds(lo, n)]

            def keys(i, par, blk):
                pe.wait_ge(s["x2_done"], i * 2 + FREE)
                for c in range(NC):
                    for w, h in HL:
                        last = mm(pD[:, 0:BT], WH[par][:, KT, w, c, :], half(h, c, blk * BT, BT),
                                  start=(c == 0 and w + h == 0), stop=(c == NC - 1 and w == 1))
                last.then_inc(s["k_done"], 1)

            def query(i, par, blk, g):
                pe.wait_ge(s["q_lo"], i * 2 + FREE)
                for c in range(NC):
                    for w, h in HL:
                        last = mm(pQ[g // 2][:, :].rearrange("p (b g t) -> p b g t", b=BB, g=2)[:, :, g % 2, :],
                                  WH[par][:, g, w, c, :],
                                  half(h, c, blk * BT, BT).rearrange("p (b t) -> p b t", b=BB),
                                  start=(c == 0 and w + h == 0), stop=(c == NC - 1 and w == 1))
                if g % 2:
                    last.then_inc(s["q_done"], 1)

            def transposes(i):
                pe.wait_ge(s["p_lo"], i + FREE)
                pe.wait_ge(s["x2_done"], i * 2 + FREE)
                for b in range(BB):
                    last = nc.tensor.transpose(pT16[:, b * P:(b + 1) * P],
                                               PST[:, b, :, :].rearrange("p h t -> p (h t)"), ident16[:, :])
                last.then_inc(s["t_done"], 1)

            def values(i, par, blk, tiles_done):
                pe.wait_ge(s["v_lo"], i + FREE)
                if tiles_done is not None:
                    pe.wait_ge(s["w_lo"], tiles_done + FREE)
                for n in range(BTILES):
                    for c in range(NC):
                        for h, w in HL:
                            last = mm(pKV[:, n * D:(n + 1) * D], half(h, c, blk * BT + n * P, P),
                                      WH[par][:, VT, w, c, :],
                                      start=(c == 0 and w + h == 0), stop=(c == NC - 1 and h == 1))
                last.then_inc(s["v_done"], 1)

            def attend(i):
                pe.wait_ge(s["v_stacked"], i * (16 * VDMAS) + FREE_DMA)
                pe.wait_ge(s["pt_copied"], i + 1)
                pe.wait_ge(s["a_lo"], i * 2 + FREE)
                for b in range(BB):
                    last = mm(pA[b // TB][:, :].rearrange("p (g b t) -> p b g t", g=G, b=TB)[:, b % TB, :, :],
                              VST[:, b, :], PT[:, b, :].rearrange("p (g t) -> p g t", g=G),
                              start=True, stop=True)
                    if b % TB == TB - 1:
                        last.then_inc(s["a_done"], 1)

            def scores(i):
                pe.wait_ge(s["k_lo"], i + 1)
                pe.wait_ge(s["q_lo"], i * 2 + 2 + FREE)
                pe.wait_ge(s["s_read"], i + FREE)
                for b in range(BB):
                    q = [h[:, b, :, :].rearrange("p g t -> p (g t)") for h in (QH, QL)]
                    mm(pS[:, b * 2 * S:(b + 1) * 2 * S], q[0], KHL[:, b, :, :].rearrange("p h t -> p (h t)"),
                       start=True, stop=False)
                    last = mm(pS[:, b * 2 * S:b * 2 * S + S], q[1], KHL[:, b, 0, :], start=False, stop=True)
                last.then_inc(s["s_done"], 1)

            def dense(i, par, n):
                pe.wait_ge(s["k_lo"], i + 1) if n == 0 and not isinstance(i, int) else None
                pe.wait_ge(s["a_lo"], i * 2 + (n + 1) + FREE)
                for g in range(G):
                    for a, w in HL:
                        last = mm([pD, pT][n][:, :], (AH, AL)[a][:, g, n * P:(n + 1) * P],
                                  WH[par][:, DT:WT, w, g, :],
                                  start=(g == 0 and a + w == 0), stop=(g == G - 1 and a == 1))
                last.then_inc(s["d_done"], 1)

            def step(i, par, before, blk, prep):
                values(i, par, blk, None if prep is None else prep[0])
                keys(i, par, blk)
                query(i, par, blk, 0)
                query(i, par, blk, 1)
                transposes(i)
                query(i, par, blk, 2)
                attend(i)
                query(i, par, blk, 3)
                if prep is not None:
                    weight_tile(prep[0], i)
                dense(i, before, 0)
                scores(i)
                dense(i, before, 1)

            def first(i, par, pair):
                pe.wait_ge(s["w_lo"], pair * (2 * WT) + (par + 1) * WT + FREE)
                step(i, par, 1 - par, 0, None)

            pe.wait_ge(s["pool_turn"], POOL_TURNS)
            pe.wait_ge(s["dense_zeroed"], 1)
            steps(pe, first, lambda i, par, blk, prep: step(i, par, par, blk, prep))
            end = KV * BLOCKS
            transposes(end)
            attend(end)
            dense(end, 1, 0)
            dense(end, 1, 1)

            def scaled(n, m):
                pe.wait_ge(s["xs_ready"], n + 1)
                for c in range(NC):
                    last = nc.tensor.transpose(pQ[m][:, c * P:(c + 1) * P], XS[m][:, c * P:(c + 1) * P], ident[:, :])
                last.then_inc(s["xt_t"], 1)

            def low_rank_t(n, m):
                pe.wait_ge(s["low_lo"], n + 1)
                nc.tensor.transpose(pT16[:, 0:P], LOWS[m].rearrange("p h t -> p (h t)"), ident16[:, :]
                                    ).then_inc(s["low_t"], 1)

            def low_products(n, m):
                pe.wait_ge(s["m_lo"], 3)
                pe.wait_ge(s["xt_lo"], n + 1)
                if not isinstance(n, int) or n >= 2:
                    pe.wait_ge(s["low_full"], n)
                for c in range(NC):
                    for h, w in HL:
                        last = mm((pS, pKV)[m][:, 0:NLAB * R], XTHL[m][:, h, c, :], LAHL[:, w, c, :],
                                  start=(c == 0 and w + h == 0), stop=(c == NC - 1 and h == 1))
                last.then_inc(s["low_done"], 1)

            def full_products(n, m):
                if not isinstance(n, int) or n >= 2:
                    pe.wait_ge(s["ot_ready"], n - 1 + FREE)
                for c in range(NC):
                    for h, w in HL:
                        last = mm(pA[m][:, :], XTHL[m][:, h, c, :], MHL[:, w, c, :],
                                  start=(c == 0 and w + h == 0), stop=(c == NC - 1 and h == 1))
                last.then_inc(s["y_done"], 1)

            def low_product(n, m):
                pe.wait_ge(s["lowt_copied"], n + 1)
                pe.wait_ge(s["yb_read"], n + FREE)
                mm(pD[:, :], LOWT[m], BST, start=True, stop=True).then_inc(s["yb_done"], 1)

            tail(pe, scaled, low_rank_t, low_products, low_product, full_products)


_INS = ["x", "itok_B_0_15", "itok_B_0_2", "L0_cond_weights", "L0_attn_w_qkv", "L0_attn_w_dense", "L0_cond2_W",
        "L0_cond2_lora_A", "L0_cond2_lora_B_w", "L0_ffn_qweight", "L0_ffn_scale", "L0_ffn_zero_point", "L0_ffn_bias"]


def kernel(**inputs):
    import numpy as np
    import concourse.bacc as bacc
    from concourse.bass_utils import run_bass_kernel_spmd

    nc = bacc.Bacc("TRN2", target_bir_lowering=False, num_devices=1)
    arrays, args = {}, []
    for name in _INS:
        a = np.ascontiguousarray(inputs[name])
        arrays[f"in_{name}"] = a
        args.append(nc.dram_tensor(f"in_{name}", a.shape, mybir.dt.from_np(a.dtype), kind="ExternalInput").ap())
    shape = inputs["x"].shape
    args.append(nc.dram_tensor("out", shape, mybir.dt.float32, kind="ExternalOutput").ap())
    adaln_attention_ffn_kernel(nc, *args)
    r = run_bass_kernel_spmd(nc, [arrays], core_ids=[0])
    return r.results[0]["out"]
```

```python
from contextlib import ExitStack

import concourse.bass as bass
from concourse import mybir
from concourse.alu_op_type import AluOpType as ALU


def adaln_attention_ffn_kernel(
    nc: bass.Bass,
    x: bass.AP,
    cond_index: bass.AP,
    label_index: bass.AP,
    w_cond: bass.AP,
    w_qkv: bass.AP,
    w_dense: bass.AP,
    w_base: bass.AP,
    lora_a: bass.AP,
    lora_b: bass.AP,
    q_ffn: bass.AP,
    ffn_scale: bass.AP,
    ffn_zero: bass.AP,
    ffn_bias: bass.AP,
    out: bass.AP,
):
    f32, f16, i32 = mybir.dt.float32, mybir.dt.float16, mybir.dt.int32
    ACT = mybir.ActivationFunctionType
    AX = mybir.AxisListType
    RED = bass.bass_isa.ReduceOp

    P = 128
    B, S, E = x.shape
    NCOND = w_cond.shape[0]
    NLAB, _, R = lora_a.shape
    HEADS, KV, D = 32, 8, 128
    G = HEADS // KV
    NC = E // P
    TOK = B * S
    TILES = TOK // P
    TB = P // S
    BB = 8
    BT = BB * S
    BTILES = BT // P
    BLOCKS = B // BB
    WT = G + 2 + NC
    KT, VT, DT = G, G + 1, G + 2
    PREP_AT = BLOCKS - WT
    ROWS_FROM = TILES - 2 * BTILES
    VDMAS = TB * 4

    IDENTS_TURN, POOL_TURNS = 3, 10
    SPLIT = 2.0 ** 15
    EVAC = 2.0 ** -24
    WEIGHTS_IN = 4 * 16
    MASKED = -3.0e38

    x_t = x.rearrange("(n a) s e -> (a s) n e", a=TB)
    out_t = out.rearrange("(n a) s e -> n (a s) e", a=TB)
    gathered = nc.dram_tensor("gathered", [B, S * S], f32, kind="Internal").ap()

    ctx = ExitStack()
    with ctx:
        def sb(name, shape, dt=f32):
            return ctx.enter_context(nc.sbuf_tensor(name, shape, dt))

        def pb(name, shape, dt=f32):
            return ctx.enter_context(nc.psum_tensor(name, shape, dt))

        def sem(name):
            return ctx.enter_context(nc.semaphore(name))

        X2 = sb("X2", [P, TILES, E])
        CH = sb("CH", [P, NC, TOK], f16)
        CL = sb("CL", [P, NC, TOK], f16)
        WN = [sb(f"WN{p}", [P, WT, E]) for p in range(2)]
        WH = [w[:, :, :].bitcast(f16).rearrange("p r (h c d) -> p r h c d", h=2, c=NC) for w in WN]
        ST = sb("ST", [P, E])
        QH = sb("QH", [P, BB, G, S], f16)
        QL = sb("QL", [P, BB, G, S], f16)
        KHL = sb("KHL", [P, BB, 2, S], f16)
        VHL = sb("VHL", [P, BTILES, 2, D], f16)
        VST = sb("VST", [P, BB, D], f16)
        PST = sb("PST", [P, BB, 4, S], f16)
        PT = sb("PT", [P, BB, P], f16)
        AH = sb("AH", [P, G, BT], f16)
        AL = sb("AL", [P, G, BT], f16)
        S1 = sb("S1", [P, BB, S])
        S2 = sb("S2", [P, BB, S])
        PR = sb("PR", [P, BB, S])
        mask = sb("mask", [P, S])
        ident = sb("ident", [P, P])
        ident16 = sb("ident16", [P, P], f16)
        smax = sb("smax", [P, BB])
        ssum = sb("ssum", [P, BB])
        srec = sb("srec", [P, BB])
        M = sb("M", [P, NC, E])
        LA = sb("LA", [P, NC, NLAB, R])
        LB = sb("LB", [P, E])
        bias = sb("bias", [P, E])
        onehot = sb("onehot", [P, TILES, NLAB])
        xtab = sb("xtab", [P, 4, TILES])
        unscale = sb("unscale", [P, 2, TILES])
        fsum = sb("fsum", [P, 16])
        wts = [sb(f"wts{p}", [P, WT]) for p in range(2)]
        label = sb("label", [P, TILES, TB], i32)
        cidx = sb("cidx", [P, 1], i32)
        xmaxs = sb("xmaxs", [P, 10])
        wmaxs = sb("wmaxs", [P, WT // 2])
        bounds = sb("bounds", [P, 8])
        wsc = [sb(f"wsc{p}", [P, 12]) for p in range(2)]
        fsc = sb("fsc", [P, 2])

        chf = CH[:, :, :].rearrange("p c t -> p (c t)").bitcast(f32)
        wbase_n = chf[:, 0:NC * E].rearrange("p (c e) -> p c e", c=NC)
        wffn_f = chf[:, NC * E:2 * NC * E].rearrange("p (c e) -> p c e", c=NC)
        wffn_t = chf[:, 2 * NC * E:3 * NC * E].rearrange("p (c e) -> p c e", c=NC)
        wffn_q = chf[:, 3 * NC * E:4 * NC * E].bitcast(i32).rearrange("p (c e) -> p c e", c=NC)
        clf = CL[:, :, :].rearrange("p c t -> p (c t)").bitcast(f32)
        lorab_n = clf[:, 0:NC * R].rearrange("p (c r) -> p c r", c=NC)
        lorab_4 = clf[:, 512:512 + NC * P].rearrange("p (c j r) -> p c j r", c=NC, j=4)
        wcond_n = clf[:, 256:384]
        gath = clf[:, 2048:2048 + S * S]
        wn1 = WN[1][:, :, :].rearrange("p r e -> p (r e)")
        bd = wn1[:, 0:TILES * P].rearrange("p (n t) -> p n t", n=TILES)
        at = {"c": 0, "w": 0}
        room = {"c": clf, "w": WN[0][:, :, :].rearrange("p r e -> p (r e)")}

        def last(*shape, dt=f32, where="c"):
            n = 1
            for k in shape:
                n *= k
            words = n // 2 if dt == f16 else n
            ap = room[where][:, at[where]:at[where] + words]
            at[where] += words
            ap = ap.bitcast(f16) if dt == f16 else ap
            if len(shape) == 3:
                ap = ap.rearrange("p (h c e) -> p h c e", h=shape[0], c=shape[1])
            return ap.rearrange("p (c e) -> p c e", c=shape[0]) if len(shape) == 2 else ap

        MHL = last(2, NC, E, dt=f16, where="w")
        LAHL = last(2, NC, NLAB * R, dt=f16, where="w")
        BST = last(E, dt=f16, where="w")
        XS = [last(E, where="w") for _ in range(2)]
        XTHL = [last(2, NC, P, dt=f16, where="w") for _ in range(2)]
        XB = [last(E) for _ in range(2)]
        OT = [last(E) for _ in range(2)]
        LOWM = last(NLAB, R)
        LOWF = [last(R) for _ in range(2)]
        LOWS = [last(4, R, dt=f16) for _ in range(2)]
        LOWT = [last(P, dt=f16) for _ in range(2)]
        assert at["c"] <= NC * TOK // 2 and at["w"] <= WT * E

        pQ = [pb(f"pQ{n}", [P, 512]) for n in range(2)]
        pKV = pb("pKV", [P, 512])
        pS = pb("pS", [P, 512])
        pT = pb("pT", [P, 512])
        pA = [pb(f"pA{n}", [P, 512]) for n in range(2)]
        pD = pb("pD", [P, 512])
        pC = [pS, pT, *pA]
        pW = [pQ[1], pKV, pD, pQ[0]]
        pT16 = pT[:, :].bitcast(f16)

        names = """ffnw_in small_in la_in cond_in gath_in gath_out bd_in wn_in v_stacked
            pool_turn chain ffn_ready ffn_t ffn_tc m_done m_copied
            xmax_ready cscale_ready c_done c_hi c_lo onehot_ready
            stage_full w_t w_hi w_lo wscale_ready wmax_part wmax_ready wmax_all xmax_all
            k_done q_done v_done s_done t_done a_done d_done
            k_hi k_lo q_hi q_lo v_hi v_lo pt_copied a_hi a_lo s_read s_sub exp_done p_full p_hi p_lo x2_done
            x2_max x2_scaled f_max f_all lb4_ready f_scaled m_hi m_lo xs_ready xb_ready xt_t xt_hi xt_lo y_done
            low_done low_full low_hi low_lo low_t lowt_copied yb_done yb_read ot_ready""".split()
        s = {n: sem(n) for n in names}
        XPARTS = 8
        x_in = [sem(f"x_in{n}") for n in range(XPARTS)]
        out_done = [sem(f"out_done{m}") for m in range(2)]
        FREE, FREE_DMA = 1, 16

        def half_of(par, r, h):
            if isinstance(r, int):
                return WH[par][:, r, h, :, :]
            return WH[par][:, bass.ds(r, 1), h, :, :].rearrange("p o c d -> p (o c) d")

        def two_heads(q, n):
            return q[:, :, 2 * n:2 * n + 2, :].rearrange("p b g t -> p b (g t)")

        def tile_of(x, n):
            return x[:, bass.ds(n, 1), :].rearrange("p o e -> p (o e)")

        def chunks(ap):
            return ap.rearrange("p (c d) -> p c d", c=NC)

        def full_bank(n, m):
            return pKV if isinstance(n, int) and n == 0 else pA[m]

        def low_bank(n, m):
            return pS if m == 0 or (isinstance(n, int) and n == 1) else pKV

        block = ctx.enter_context(nc.Block())

        def steps(eng, begin, first, rest, before_last=None, final=None):
            def head(pair, par):
                base = pair * (2 * BLOCKS) + par * BLOCKS
                with eng.Fori(1, PREP_AT) as blk:
                    rest(blk + base, par, blk, None)
                with eng.Fori(PREP_AT, BLOCKS) as blk:
                    rest(blk + base, par, blk, (blk + (pair * (2 * WT) + (par + 1) * WT - PREP_AT),
                                                pair * 2 + (par + 2)))
                first(base + BLOCKS, 1 - par, pair)

            begin()
            with eng.Fori(0, KV // 2 - 1) as pair:
                head(pair, 0)
                head(pair, 1)
            head(KV // 2 - 1, 0)
            if before_last is not None:
                before_last()
            with eng.Fori(1, BLOCKS if final is None else BLOCKS - 1) as blk:
                rest(blk + (KV - 1) * BLOCKS, 1, blk, None)
            if final is not None:
                final()

        def tail(eng, start, ahead, before, here, after, last=None):
            def call(f, n, m):
                if f is not None:
                    f(n, m)

            def pair_of(pair):
                for k in range(2):
                    n = pair * 2 + (k + 1)
                    call(before, n - 1, k)
                    call(ahead, n + 1, k)
                    call(here, n, 1 - k)
                    call(after, n - 1, k)
                    call(last, n, 1 - k)

            start()
            pair_of(0)
            with eng.Fori(1, TILES // 2 - 2) as pair:
                pair_of(pair)
            pair_of(TILES // 2 - 2)
            call(before, TILES - 2, 0)
            call(here, TILES - 1, 1)
            call(after, TILES - 2, 0)
            call(last, TILES - 1, 1)
            call(before, TILES - 1, 1)
            call(after, TILES - 1, 1)

        @block.sync
        def _(sp):
            sp.dma_start(cidx[:, :], cond_index.rearrange("(b o) -> b o", o=1)).then_inc(s["cond_in"], 16)
            sp.nop().then_inc(s["v_stacked"], FREE_DMA)
            for m in range(2):
                sp.nop().then_inc(out_done[m], FREE_DMA)
            sp.dma_start(wffn_q, q_ffn.rearrange("(c p) e -> p c e", p=P)).then_inc(s["ffnw_in"], 16)
            sp.dma_start(wbase_n, w_base.rearrange("(c p) e -> p c e", p=P)).then_inc(s["ffnw_in"], 16)
            sp.dma_start(lorab_n, lora_b.rearrange("(c p) r -> p c r", p=P)).then_inc(s["ffnw_in"], 16)

            def load_weights(par, kv):
                q = w_qkv[bass.ds(kv * (G * D), G * D), :]
                k = w_qkv[bass.ds(kv * D + HEADS * D, D), :]
                v = w_qkv[bass.ds(kv * D + (HEADS + KV) * D, D), :]
                d = w_dense[:, bass.ds(kv * (G * D), G * D)]
                sp.dma_start(WN[par][:, 0:G, :], q.rearrange("(g p) e -> p g e", p=P)).then_inc(s["wn_in"], 16)
                sp.dma_start(WN[par][:, KT, :], k).then_inc(s["wn_in"], 16)
                sp.dma_start(WN[par][:, VT, :], v).then_inc(s["wn_in"], 16)
                sp.dma_start(WN[par][:, DT:WT, :], d.rearrange("(c p) e -> p c e", p=P)).then_inc(s["wn_in"], 16)

            def load_x(parts):
                for n in parts:
                    part = slice(n * TILES // XPARTS, (n + 1) * TILES // XPARTS)
                    sp.dma_start(X2[:, part, :], x_t[:, part, :]).then_inc(x_in[n], 16)

            load_x(range(2))
            sp.wait_ge(s["gath_in"], 16)
            sp.dma_start(gathered, gath).then_inc(s["gath_out"], 16)
            load_x(range(2, XPARTS))
            sp.wait_ge(s["gath_out"], 16)
            sp.wait_ge(s["pool_turn"], IDENTS_TURN + 1)
            src = gathered.rearrange("(n a) (c d) -> a c n d", a=TB, c=S)
            for a in range(TB):
                sp.dma_start(bd[a * S:(a + 1) * S, :, a * S:(a + 1) * S], src[a]).then_inc(s["bd_in"], 16)
            load_weights(0, 0)

            def stack_values(i):
                sp.wait_ge(s["v_lo"], i + 1 + FREE)
                if not isinstance(i, int) or i > 0:
                    sp.wait_ge(s["a_done"], (i - 1) * 2 + 2)
                for a in range(TB):
                    for j in range(4):
                        sp.dma_start(VST[j * S:(j + 1) * S, a::TB, :],
                                     VHL[a * S:(a + 1) * S, :, j // 2, :]).then_inc(s["v_stacked"], 16)

            def begin():
                stack_values(0)
                sp.wait_ge(s["c_lo"], TILES)
                load_weights(1, 1)

            def first(i, par, pair):
                stack_values(i)
                if not isinstance(pair, int):
                    kv = pair * 2 + (2 if par == 1 else 3)
                    sp.wait_ge(s["x2_done"], i * 2 + FREE)
                    load_weights(1 - par, kv)

            def rest(i, par, blk, prep):
                stack_values(i)

            steps(sp, begin, first, rest)
            with sp.Fori(0, TILES // 2) as pair:
                for n in range(2):
                    sp.wait_ge(s["ot_ready"], pair * 2 + n + 1 + FREE)
                    sp.dma_start(out_t[pair * 2 + n, :, :], OT[n]).then_inc(out_done[n], 16)
            for m in range(2):
                sp.wait_ge(out_done[m], 16 * TILES // 2 + FREE_DMA)

        @block.gpsimd
        def _(pool):
            turns = [0]

            def turn(ins):
                turns[0] += 1
                ins.then_inc(s["pool_turn"], 1)
                pool.wait_ge(s["pool_turn"], turns[0])

            turn(pool.memset(ident[:, :], 0.0))
            turn(pool.affine_select(out=ident[:, :], in_=ident[:, :], compare_op=ALU.not_equal, fill=1.0, base=0,
                                    pattern=[[-1, P]], channel_multiplier=1))
            turn(pool.tensor_copy(ident16[:, :], ident[:, :]))
            assert turns[0] == IDENTS_TURN
            pool.wait_ge(s["cond_in"], 16)
            pool.indirect_dma_start(gath, None, w_cond.rearrange("n c d -> n (c d)"),
                                    bass.IndirectOffsetOnAxis(ap=cidx[:, 0:1], axis=0)).then_inc(s["gath_in"], 16)
            turn(pool.memset(wn1, 0.0))
            pool.wait_ge(s["gath_in"], 16)
            turn(pool.memset(mask[:, :], 0.0))
            for q in range(4):
                m = mask[q * S:(q + 1) * S, :]
                turn(pool.affine_select(out=m, in_=m, compare_op=ALU.is_ge, fill=1.0, base=0,
                                        pattern=[[-1, S]], channel_multiplier=1))
            turn(pool.tensor_scalar(mask[:, :], mask[:, :], MASKED, None, ALU.mult))
            assert turns[0] == POOL_TURNS

            def stage_tile(par, r, n):
                pool.wait_ge(s["w_t"], n)
                src = WN[par][:, bass.ds(r, 1), :].rearrange("p o e -> p (o e)")
                pool.tensor_copy(ST[:, :], src).then_inc(s["stage_full"], 1)

            pool.wait_ge(s["xmax_ready"], 1)
            pool.partition_all_reduce(bounds[:, 0:2], xmaxs[:, 8:10], P, RED.absmax).then_inc(s["xmax_all"], 1)
            pool.wait_ge(s["xmax_all"], 1)
            pool.wait_ge(s["wmax_ready"], 2)
            pool.partition_all_reduce(wsc[0][:, 0:2], wsc[0][:, 6:8], P, RED.absmax).then_inc(s["wmax_all"], 1)
            pool.wait_ge(s["wmax_all"], 1)
            pool.wait_ge(s["f_max"], 3)
            pool.partition_all_reduce(fsum[:, 3:6], fsum[:, 0:3], P, RED.absmax).then_inc(s["f_all"], 1)
            pool.wait_ge(s["f_all"], 1)

            for kv in range(KV - 1):
                sc = wsc[(kv + 1) % 2]
                pool.wait_ge(s["wmax_ready"], 2 * (kv + 2))
                pool.partition_all_reduce(sc[:, 0:2], sc[:, 6:8], P, RED.absmax).then_inc(s["wmax_all"], 1)
                pool.wait_ge(s["wmax_all"], kv + 2)
                with pool.Fori(0, WT) as r:
                    stage_tile((kv + 1) % 2, r, (kv + 1) * WT + r)

            pool.wait_ge(s["x2_done"], 2 * KV * BLOCKS + FREE)
            for n in range(2):
                pool.tensor_tensor(XB[n], X2[:, n, :], bias[:, :], ALU.add).then_inc(s["xb_ready"], 1)
            with pool.Fori(1, TILES // 2) as pair:
                for m in range(2):
                    n = pair * 2 + m
                    pool.wait_ge(s["ot_ready"], n - 1 + FREE)
                    pool.tensor_tensor(XB[m], tile_of(X2, n), bias[:, :], ALU.add).then_inc(s["xb_ready"], 1)

        @block.scalar
        def _(act):
            act.dma_start(wcond_n, w_cond.rearrange("n c d -> (n c d)").rearrange("(p f) -> p f", p=P)).then_inc(s["small_in"], 16)
            act.dma_start(fsc[:, 0:1], ffn_scale.rearrange("(o n) -> o n", o=1).to_broadcast([P, 1])).then_inc(s["small_in"], 16)
            act.dma_start(fsc[:, 1:2], ffn_zero.rearrange("(o n) -> o n", o=1).to_broadcast([P, 1])).then_inc(s["small_in"], 16)
            act.dma_start(label[:, :, :].rearrange("p n a -> p (n a)"),
                          label_index.rearrange("(o b) -> o b", o=1).to_broadcast([P, B])).then_inc(s["small_in"], 16)
            for c in range(NC):
                act.dma_start(LA[:, c, :, :], lora_a[:, c * P:(c + 1) * P, :].rearrange("l p r -> p l r")).then_inc(s["la_in"], 16)
            act.dma_start(bias[:, :], ffn_bias.rearrange("(o n) -> o n", o=1).to_broadcast([P, E])).then_inc(s["la_in"], 16)

            for c in range(NC):
                act.wait_ge(s["ffn_t"], c + 1)
                act.activation(wffn_t[:, :, c * P:(c + 1) * P], chunks(pQ[c % 2][:, :]), ACT.Copy).then_inc(s["ffn_tc"], 1)

            def weight_hi(par, r, n):
                act.wait_ge(s["w_t"], n + 1)
                act.activation(half_of(par, r, 0), chunks(pKV[:, :]), ACT.Copy,
                               scale=wts[par][:, bass.ds(r, 1)]).then_inc(s["w_hi"], 1)

            for c in range(NC):
                act.wait_ge(s["m_done"], c + 1)
                act.activation(M[:, c, :], pC[c][:, :], ACT.Copy).then_inc(s["m_copied"], 1)
            act.wait_ge(s["m_done"], NC + 1)
            act.activation(LB[:, :], pQ[0][:, :], ACT.Copy, scale=0.5).then_inc(s["m_copied"], 1)
            act.wait_ge(s["cscale_ready"], 1)
            def c_high(n, m):
                act.wait_ge(s["c_done"], n + 1)
                act.activation(CH[:, :, bass.ds(n * P, P)], chunks(pC[m][:, :]), ACT.Copy,
                               scale=bounds[:, 6:7]).then_inc(s["c_hi"], 1)

            def first_weight_hi(r):
                act.wait_ge(s["w_t"], r + 1)
                act.activation(half_of(0, r, 0), chunks(pW[r % 4][:, :]), ACT.Copy,
                               scale=wts[0][:, r:r + 1]).then_inc(s["w_hi"], 1)

            with act.Fori(0, TILES // 4 - 1) as four:
                for m in range(4):
                    c_high(four * 4 + m, m)
            act.wait_ge(s["wscale_ready"], 1)
            for r in range(4):
                first_weight_hi(r)
            for m in range(4):
                c_high(TILES - 4 + m, m)
            for r in range(4, WT):
                first_weight_hi(r)

            def values(i):
                act.wait_ge(s["v_done"], i + 1)
                act.wait_ge(s["v_stacked"], i * (16 * VDMAS) + FREE_DMA)
                act.activation(VHL[:, :, 0, :], pKV[:, 0:BTILES * D].rearrange("p (n d) -> p n d", n=BTILES),
                               ACT.Copy, scale=EVAC).then_inc(s["v_hi"], 1)

            def keys(i):
                act.wait_ge(s["k_done"], i + 1)
                act.activation(KHL[:, :, 0, :], pD[:, 0:BT].rearrange("p (b t) -> p b t", b=BB), ACT.Copy,
                               scale=EVAC).then_inc(s["k_hi"], 1)

            def queries(i, n):
                act.wait_ge(s["q_done"], i * 2 + (n + 1))
                act.activation(two_heads(QH, n), pQ[n][:, :].rearrange("p (b n) -> p b n", b=BB),
                               ACT.Copy, scale=EVAC).then_inc(s["q_hi"], 1)

            def attend(i):
                act.wait_ge(s["t_done"], i + 1)
                for n in range(2):
                    half_b = slice(n * TB, (n + 1) * TB)
                    act.activation(PT[:, half_b, :], pT16[:, n * TB * P:(n + 1) * TB * P].rearrange(
                        "p (b t) -> p b t", b=TB), ACT.Copy).then_inc(s["pt_copied"], 1)

            def attended(i):
                for n in range(2):
                    act.wait_ge(s["a_done"], i * 2 + (n + 1))
                    act.activation(AH[:, :, n * P:(n + 1) * P], pA[n][:, :].rearrange("p (g n) -> p g n", g=G),
                                   ACT.Copy).then_inc(s["a_hi"], 1)

            def softmax(i, par, before_exp, after_exp):
                if before_exp is not None:
                    before_exp()
                act.wait_ge(s["s_sub"], i + 1)
                act.activation(S2[:, :, :], S1[:, :, :], ACT.Exp, scale=wsc[par][:, 9:10]).then_inc(s["exp_done"], 1)
                if after_exp is not None:
                    after_exp()
                act.wait_ge(s["p_full"], i + 1)
                act.activation(PST[:, :, 0::2, :], PR[:, :, :].unsqueeze(2).to_broadcast([P, BB, 2, S]),
                               ACT.Copy).then_inc(s["p_hi"], 1)

            def step(i, par, blk, prep, before_exp=None, after_exp=None):
                values(i)
                keys(i)
                queries(i, 0)
                if not isinstance(i, int) or i > 0:
                    attend(i - 1)
                    attended(i - 1)
                queries(i, 1)
                if prep is not None:
                    act.wait_ge(s["wscale_ready"], prep[1])
                    weight_hi(1 - par, blk - PREP_AT, prep[0])
                softmax(i, par, before_exp, after_exp)

            def folded_hi():
                act.wait_ge(s["f_scaled"], 1)
                act.activation(MHL[:, 0, :, :], M[:, :, :], ACT.Copy, scale=fsum[:, 12:13]).then_inc(s["m_hi"], 1)
                act.activation(LAHL[:, 0, :, :], LA[:, :, :, :].rearrange("p c l r -> p c (l r)"), ACT.Copy,
                               scale=fsum[:, 13:14]).then_inc(s["m_hi"], 1)
                act.activation(BST, LB[:, :], ACT.Copy, scale=fsum[:, 14:15]).then_inc(s["m_hi"], 1)

            def scale_rows(n, m):
                act.wait_ge(s["x2_scaled"], 1 if isinstance(n, int) and n < ROWS_FROM else 2)
                act.activation(XS[m], tile_of(X2, n), ACT.Copy, scale=xtab[:, 3, bass.ds(n, 1)]).then_inc(s["xs_ready"], 1)

            def transposed(n, m):
                act.wait_ge(s["xt_t"], n + 1)
                act.activation(XTHL[m][:, 0, :, :], chunks(pQ[m][:, :]), ACT.Copy).then_inc(s["xt_hi"], 1)

            def scale_first():
                for n in range(2):
                    scale_rows(n, n)

            steps(act, lambda: step(0, 0, 0, None), lambda i, par, pair: step(i, par, 0, None), step, folded_hi,
                  lambda: step(KV * BLOCKS - 1, 1, BLOCKS - 1, None, scale_first, lambda: transposed(0, 0)))

            def start():
                transposed(1, 1)
                attend(KV * BLOCKS - 1)
                attended(KV * BLOCKS - 1)
                low_rank(0, 0)
                scale_next(0, 0)

            def scale_next(n, m):
                if not isinstance(n, int) or n + 2 < TILES:
                    scale_rows(n + 2, m)

            def low_rank(n, m):
                act.wait_ge(s["low_full"], n + 1)
                act.activation(LOWS[m][:, 0::2, :], LOWF[m].unsqueeze(1).to_broadcast([P, 2, R]),
                               ACT.Copy).then_inc(s["low_hi"], 1)

            def low_rank_t(n, m):
                act.wait_ge(s["low_t"], n + 1)
                act.activation(LOWT[m], pT16[:, 0:P], ACT.Copy).then_inc(s["lowt_copied"], 1)

            tail(act, start, transposed, low_rank_t, low_rank, None, scale_next)

        @block.vector
        def _(dve):
            def chained(instructions, base):
                n = 0
                for ins in instructions:
                    n += 1
                    ins.then_inc(s["chain"], 1)
                    dve.wait_ge(s["chain"], base + n)
                return n

            def powers(src, power, inverse):
                yield dve.tensor_scalar(power, src, 1e-30, 2.0, ALU.max, ALU.mult)
                yield dve.tensor_scalar(power.bitcast(i32), power.bitcast(i32), 0x7F800000, None, ALU.bitwise_and)
                yield dve.tensor_scalar(inverse.bitcast(i32), power.bitcast(i32), -1.0, float(254 << 23),
                                        ALU.mult, ALU.add)

            def max_pair(par, k):
                src = WN[par][:, bass.ds(k * 2, 2), :].rearrange("p r e -> p (r e)")
                dve.tensor_reduce(wmaxs[:, bass.ds(k, 1)], src, AX.X, ALU.max, apply_absolute_value=True
                                  ).then_inc(s["wmax_part"], 1)

            def head_max(par, n):
                dve.wait_ge(s["wmax_part"], n)
                dve.tensor_reduce(wsc[par][:, 6:7], wmaxs[:, 0:DT // 2], AX.X, ALU.max).then_inc(s["wmax_ready"], 1)
                dve.tensor_reduce(wsc[par][:, 7:8], wmaxs[:, DT // 2:WT // 2], AX.X, ALU.max).then_inc(s["wmax_ready"], 1)

            def tile_scales(par):
                sc = wsc[par]
                yield from powers(sc[:, 0:2], sc[:, 2:4], sc[:, 4:6])
                for k, (lo, hi) in enumerate(((0, DT), (DT, WT))):
                    ins = dve.tensor_scalar(wts[par][:, lo:hi], sc[:, 4 + k:5 + k].to_broadcast([P, hi - lo]),
                                            SPLIT, None, ALU.mult)
                    yield ins

            def stage_scales(par):
                sc = wsc[par]
                yield dve.tensor_scalar(sc[:, 8:9], sc[:, 2:3], bounds[:, 4:5], E / SPLIT, ALU.mult, ALU.mult)
                yield dve.scalar_tensor_tensor(sc[:, 9:10], sc[:, 8:9], float(D) ** -0.5, sc[:, 8:9],
                                               ALU.mult, ALU.mult)
                yield dve.tensor_scalar(sc[:, 10:11], sc[:, 3:4], sc[:, 8:9], 1.0 / SPLIT, ALU.mult, ALU.mult)

            for name in "v_lo q_lo x2_done a_lo s_read w_lo yb_read ot_ready".split():
                dve.nop().then_inc(s[name], FREE)
            dve.wait_ge(s["ffnw_in"], 48)
            dve.wait_ge(s["small_in"], 64)
            dve.tensor_scalar(wffn_f, wffn_q, fsc[:, 1:2], fsc[:, 0:1], ALU.subtract, ALU.mult).then_inc(s["ffn_ready"], 1)
            dve.tensor_copy(lorab_4, lorab_n.unsqueeze(2).to_broadcast([P, NC, 4, R])).then_inc(s["lb4_ready"], 1)
            dve.tensor_reduce(xmaxs[:, 9:10], wcond_n, AX.X, ALU.max, apply_absolute_value=True).then_inc(s["chain"], 1)
            for l in range(NLAB):
                for a in range(TB):
                    dve.tensor_scalar(onehot[a * S:(a + 1) * S, :, l], label[a * S:(a + 1) * S, :, a], float(l), EVAC,
                                      ALU.is_equal, ALU.mult).then_inc(s["onehot_ready"], 1)

            def weight_lo(par, r, n):
                dve.wait_ge(s["w_hi"], n + 1)
                dve.scalar_tensor_tensor(half_of(par, r, 1), chunks(pKV[:, :]), wts[par][:, bass.ds(r, 1)],
                                         half_of(par, r, 0), ALU.mult, ALU.subtract).then_inc(s["w_lo"], 1)

            def x_max(n):
                dve.wait_ge(x_in[n], 16)
                part = slice(n * TILES // XPARTS, (n + 1) * TILES // XPARTS)
                dve.tensor_reduce(xmaxs[:, n:n + 1], X2[:, part, :].rearrange("p n e -> p (n e)"),
                                  AX.X, ALU.max, apply_absolute_value=True).then_inc(s["chain"], 1)

            def first_weight_lo(r):
                dve.wait_ge(s["w_hi"], r + 1)
                dve.scalar_tensor_tensor(half_of(0, r, 1), chunks(pW[r % 4][:, :]), wts[0][:, r:r + 1],
                                         half_of(0, r, 0), ALU.mult, ALU.subtract).then_inc(s["w_lo"], 1)

            for n in range(XPARTS):
                x_max(n)
            dve.wait_ge(s["chain"], 1 + XPARTS)
            dve.tensor_reduce(xmaxs[:, 8:9], xmaxs[:, 0:8], AX.X, ALU.max).then_inc(s["xmax_ready"], 1)

            def c_scale():
                yield from powers(bounds[:, 0:2], bounds[:, 2:4], xmaxs[:, 0:2])
                yield dve.tensor_scalar(bounds[:, 4:5], bounds[:, 2:3], bounds[:, 3:4], float(S), ALU.mult, ALU.mult)
                yield dve.tensor_scalar(bounds[:, 5:6].bitcast(i32), bounds[:, 4:5].bitcast(i32), -1.0,
                                        float(254 << 23), ALU.mult, ALU.add)

            dve.wait_ge(s["xmax_all"], 1)
            used = 1 + XPARTS
            used += chained(c_scale(), used)
            dve.tensor_scalar(bounds[:, 6:7], bounds[:, 5:6], SPLIT, None, ALU.mult).then_inc(s["cscale_ready"], 1)
            dve.wait_ge(s["cscale_ready"], 1)

            def c_lo(n, m):
                dve.wait_ge(s["c_hi"], n + 1)
                dve.scalar_tensor_tensor(CL[:, :, bass.ds(n * P, P)], chunks(pC[m][:, :]), bounds[:, 6:7],
                                         CH[:, :, bass.ds(n * P, P)], ALU.mult, ALU.subtract).then_inc(s["c_lo"], 1)

            fours = TILES // 4
            max_from = fours - 2 - WT // 2
            with dve.Fori(0, max_from) as four:
                for m in range(4):
                    c_lo(four * 4 + m, m)
            dve.wait_ge(s["wn_in"], WEIGHTS_IN)
            with dve.Fori(max_from, fours - 2) as four:
                for m in range(4):
                    c_lo(four * 4 + m, m)
                max_pair(0, four - max_from)
            head_max(0, WT // 2)
            for m in range(4):
                c_lo(TILES - 8 + m, m)
            dve.wait_ge(s["wmax_all"], 1)
            n_tiles = chained(tile_scales(0), used)
            dve.tensor_copy(wsc[0][:, 11:12], wts[0][:, 0:1]).then_inc(s["wscale_ready"], 1)
            n_stage = chained(stage_scales(0), used + n_tiles)
            per_head = n_tiles + n_stage
            used += per_head
            for r in range(4):
                first_weight_lo(r)
            for m in range(4):
                c_lo(TILES - 4 + m, m)
            for r in range(4, WT):
                first_weight_lo(r)

            folded = (M[:, :, :].rearrange("p c e -> p (c e)"), LA[:, :, :, :].rearrange("p c l r -> p (c l r)"),
                      LB[:, :])

            def folded_max(n):
                dve.wait_ge(s["la_in"], 16 * (NC + 1))
                dve.wait_ge(s["m_copied"], NC + 1)
                dve.tensor_reduce(fsum[:, n:n + 1], folded[n], AX.X, ALU.max, apply_absolute_value=True
                                  ).then_inc(s["f_max"], 1)

            def low(out, psum, high, done, scale=EVAC):
                dve.scalar_tensor_tensor(out, psum, scale, high, ALU.mult, ALU.subtract).then_inc(s[done], 1)

            def values(i):
                dve.wait_ge(s["v_hi"], i + 1)
                low(VHL[:, :, 1, :], pKV[:, 0:BTILES * D].rearrange("p (n d) -> p n d", n=BTILES),
                    VHL[:, :, 0, :], "v_lo")

            def keys(i):
                dve.wait_ge(s["k_hi"], i + 1)
                low(KHL[:, :, 1, :], pD[:, 0:BT].rearrange("p (b t) -> p b t", b=BB), KHL[:, :, 0, :], "k_lo")

            def queries(i, n):
                dve.wait_ge(s["q_hi"], i * 2 + (n + 1))
                low(two_heads(QL, n), pQ[n][:, :].rearrange("p (b n) -> p b n", b=BB), two_heads(QH, n), "q_lo")

            def attended(i):
                for n in range(2):
                    dve.wait_ge(s["a_hi"], i * 2 + (n + 1))
                    low(AL[:, :, n * P:(n + 1) * P], pA[n][:, :].rearrange("p (g n) -> p g n", g=G),
                        AH[:, :, n * P:(n + 1) * P], "a_lo", 1.0)

            def spread(row):
                return row.unsqueeze(2).to_broadcast([P, BB, S])

            def scores(i, base):
                dve.wait_ge(s["s_done"], i + 1)
                sc = pS[:, :].rearrange("p (b h t) -> p b h t", b=BB, h=2)
                chained([dve.tensor_tensor(S1[:, :, :], sc[:, :, 0, :],
                                           mask[:, :].unsqueeze(1).to_broadcast([P, BB, S]), ALU.add)], base)
                dve.tensor_tensor(S2[:, :, :], S1[:, :, :], sc[:, :, 1, :], ALU.add).then_inc(s["s_read"], 1)
                dve.wait_ge(s["s_read"], i + 1 + FREE)
                chained([dve.tensor_reduce(smax[:, :], S2[:, :, :], AX.X, ALU.max)], base + 1)
                dve.tensor_tensor(S1[:, :, :], S2[:, :, :], spread(smax[:, :]), ALU.subtract).then_inc(s["s_sub"], 1)

            def probabilities(i, base, meanwhile=None):
                dve.wait_ge(s["exp_done"], i + 1)
                chained([dve.tensor_reduce(ssum[:, :], S2[:, :, :], AX.X, ALU.add)], base)
                chained([dve.reciprocal(srec[:, :], ssum[:, :])], base + 1)
                dve.tensor_tensor(PR[:, :, :], S2[:, :, :], spread(srec[:, :]), ALU.mult).then_inc(s["p_full"], 1)
                if meanwhile is not None:
                    meanwhile()
                dve.wait_ge(s["p_hi"], i + 1)
                dve.tensor_tensor(PST[:, :, 1::2, :], PR[:, :, :].unsqueeze(2).to_broadcast([P, BB, 2, S]),
                                  PST[:, :, 0::2, :], ALU.subtract).then_inc(s["p_lo"], 1)

            def update(i, par, tile, n):
                dve.wait_ge(s["d_done"], i * 2 + (n + 1))
                t = X2[:, bass.ds(tile, 1), :].rearrange("p o e -> p (o e)")
                dve.scalar_tensor_tensor(t, [pD, pT][n][:, :], wsc[par][:, 10:11], t, ALU.mult, ALU.add
                                         ).then_inc(s["x2_done"], 1)

            def row_max(i, tile, n):
                dve.wait_ge(s["x2_done"], i * 2 + (n + 1) + FREE)
                dve.tensor_reduce(xtab[:, 0, bass.ds(tile, 1)], X2[:, bass.ds(tile, 1), :].rearrange("p o e -> p (o e)"),
                                  AX.X, ALU.max, apply_absolute_value=True).then_inc(s["x2_max"], 1)

            PER = 4

            def step(i, par, before, blk, prep, tile, head, loads=None, meanwhile=None):
                base = i * PER + (head + used)
                values(i)
                keys(i)
                queries(i, 0)
                if before is not None:
                    attended(i - 1)
                else:
                    folded_max(0)
                queries(i, 1)
                if before is None:
                    folded_max(1)
                    folded_max(2)
                if prep is not None:
                    weight_lo(1 - par, blk - PREP_AT, prep)
                if before is not None:
                    update(i - 1, before, tile, 0)
                scores(i, base)
                if before is not None:
                    update(i - 1, before, tile + 1, 1)
                probabilities(i, base + 2, meanwhile)
                if before == 1:
                    for n in range(2):
                        row_max(i - 1, tile + n, n)
                if loads is not None:
                    dve.wait_ge(s["wn_in"], loads)
                    max_pair(1 - par, blk - 1)

            def scaled(n, m):
                dve.wait_ge(s["xt_hi"], n + 1)
                dve.tensor_tensor(XTHL[m][:, 1, :, :], chunks(pQ[m][:, :]), XTHL[m][:, 0, :, :],
                                  ALU.subtract).then_inc(s["xt_lo"], 1)

            last_tile = (BLOCKS - 1) * BTILES
            dve.wait_ge(s["pool_turn"], POOL_TURNS)

            def head_steps(pair, par, before_it=0, meanwhile=None):
                start = pair * (2 * BLOCKS) + par * BLOCKS
                prep = pair * (2 * WT) + ((par + 1) * WT - PREP_AT)
                head = pair * (2 * per_head) + (par * per_head + before_it)
                with dve.Fori(1, PREP_AT) as blk:
                    step(blk + start, par, par, blk, None, (blk - 1) * BTILES, head, 
                         pair * (2 * WEIGHTS_IN) + (par + 2) * WEIGHTS_IN)
                head_max(1 - par, (pair * WT + (par + 2) * (WT // 2)))
                dve.wait_ge(s["wmax_all"], pair * 2 + (par + 2))
                base = (start + PREP_AT) * PER + (head + used)
                chained(tile_scales(1 - par), base)
                chained(stage_scales(1 - par), base + n_tiles)
                dve.tensor_copy(wsc[1 - par][:, 11:12], wts[1 - par][:, 0:1]).then_inc(s["wscale_ready"], 1)
                with dve.Fori(PREP_AT, BLOCKS) as blk:
                    step(blk + start, par, par, blk, blk + prep, (blk - 1) * BTILES, head + per_head)
                step(start + BLOCKS, 1 - par, par, 0, None, last_tile, head + per_head, meanwhile=meanwhile)

            step(0, 0, None, 0, None, None, 0)
            with dve.Fori(0, KV // 2 - 1) as pair:
                head_steps(pair, 0)
                head_steps(pair, 1)

            def folded_scales():
                yield from powers(fsum[:, 3:6], fsum[:, 6:9], fsum[:, 9:12])
                yield dve.tensor_scalar(fsum[:, 12:15], fsum[:, 9:12], SPLIT, None, ALU.mult)
                yield dve.tensor_tensor(fsum[:, 15:16], fsum[:, 7:8], fsum[:, 8:9], ALU.mult)

            def row_scales(lo, hi):
                yield from powers(*(xtab[:, k, lo:hi] for k in range(3)))
                yield dve.tensor_scalar(xtab[:, 3, lo:hi], xtab[:, 2, lo:hi], SPLIT, None, ALU.mult)

            def unscales():
                yield dve.tensor_scalar(unscale[:, 0, :], xtab[:, 1, :], fsum[:, 6:7], SPLIT ** -2, ALU.mult, ALU.mult)
                yield dve.tensor_scalar(unscale[:, 1, :], xtab[:, 1, :], fsum[:, 15:16], SPLIT ** -3 / EVAC,
                                        ALU.mult, ALU.mult)

            def weights_free():
                dve.wait_ge(s["d_done"], 2 * (KV - 1) * BLOCKS)
                dve.nop().then_inc(s["f_scaled"], 1)

            dve.wait_ge(s["f_all"], 1)
            n_f = chained(folded_scales(), (KV - 2) * (BLOCKS * PER + per_head) + PER + used)
            head_steps(KV // 2 - 1, 0, n_f, weights_free)
            dve.wait_ge(s["m_hi"], 1)
            dve.scalar_tensor_tensor(MHL[:, 1, :, :], M[:, :, :], fsum[:, 12:13], MHL[:, 0, :, :],
                                     ALU.mult, ALU.subtract).then_inc(s["m_lo"], 1)
            dve.wait_ge(s["m_hi"], 3)
            dve.scalar_tensor_tensor(LAHL[:, 1, :, :], LA[:, :, :, :].rearrange("p c l r -> p c (l r)"), fsum[:, 13:14],
                                     LAHL[:, 0, :, :], ALU.mult, ALU.subtract).then_inc(s["m_lo"], 1)
            half_p = slice(P // 2, P)
            dve.scalar_tensor_tensor(BST[half_p, :], LB[half_p, :], fsum[half_p, 14:15], BST[half_p, :],
                                     ALU.mult, ALU.subtract).then_inc(s["m_lo"], 1)

            with dve.Fori(1, BLOCKS - 1) as blk:
                step(blk + (KV - 1) * BLOCKS, 1, 1, blk, None, (blk - 1) * BTILES, (KV - 1) * per_head + n_f)
            dve.wait_ge(s["x2_max"], KV * BLOCKS - 2 * BTILES)
            before_last = (KV * BLOCKS - 1) * PER + (KV - 1) * per_head + n_f + used
            n_rows = chained(row_scales(0, ROWS_FROM), before_last)
            dve.nop().then_inc(s["x2_scaled"], 1)
            step(KV * BLOCKS - 1, 1, 1, BLOCKS - 1, None, ROWS_FROM, (KV - 1) * per_head + n_f + n_rows,
                 meanwhile=lambda: scaled(0, 0))
            done = before_last + n_rows + PER
            dve.wait_ge(s["q_done"], 2 * KV * BLOCKS)

            def low_rank(n, m):
                dve.wait_ge(s["low_done"], n + 1)
                which = onehot[:, bass.ds(n, 1), :].rearrange("p o l -> p (o l)").unsqueeze(2).to_broadcast([P, NLAB, R])
                chained([dve.tensor_tensor(LOWM, low_bank(n, m)[:, 0:NLAB * R].rearrange("p (l r) -> p l r", l=NLAB),
                                           which, ALU.mult)], n + low_base)
                dve.tensor_reduce(LOWF[m], LOWM.rearrange("p l r -> p r l"), AX.X, ALU.add).then_inc(s["low_full"], 1)
                dve.wait_ge(s["low_hi"], n + 1)
                dve.tensor_tensor(LOWS[m][:, 1::2, :], LOWF[m].unsqueeze(1).to_broadcast([P, 2, R]),
                                  LOWS[m][:, 0::2, :], ALU.subtract).then_inc(s["low_lo"], 1)

            low_base = done
            dve.wait_ge(s["onehot_ready"], NLAB * TB)
            scaled(1, 1)
            attended(KV * BLOCKS - 1)
            low_rank(0, 0)
            for n in range(BTILES):
                update(KV * BLOCKS - 1, 1, last_tile + n, n)
                row_max(KV * BLOCKS - 1, last_tile + n, n)
            dve.wait_ge(s["x2_max"], KV * BLOCKS)
            n_end = chained(row_scales(ROWS_FROM, TILES), done + 1)
            dve.nop().then_inc(s["x2_scaled"], 1)
            n_end += chained(unscales(), done + 1 + n_end)
            low_base += n_end

            def output(n, m):
                dve.wait_ge(s["yb_done"], n + 1)
                dve.wait_ge(s["xb_ready"], n + 1)
                dve.wait_ge(out_done[m], (n - m) * 8 + FREE_DMA)
                dve.scalar_tensor_tensor(OT[m], pD[:, :], unscale[:, 1, bass.ds(n, 1)], XB[m], ALU.mult, ALU.add
                                         ).then_inc(s["yb_read"], 1)
                dve.wait_ge(s["yb_read"], n + 1 + FREE)
                dve.wait_ge(s["y_done"], n + 1)
                dve.scalar_tensor_tensor(OT[m], full_bank(n, m)[:, :], unscale[:, 0, bass.ds(n, 1)], OT[m], ALU.mult, ALU.add
                                         ).then_inc(s["ot_ready"], 1)

            tail(dve, lambda: None, scaled, None, low_rank, output)

        @block.tensor
        def _(pe):
            mm = nc.tensor.matmul
            pe.wait_ge(s["pool_turn"], IDENTS_TURN)
            pe.wait_ge(s["ffn_ready"], 1)
            for oc in range(NC):
                if oc >= 2:
                    pe.wait_ge(s["ffn_tc"], oc - 1)
                for mc in range(NC):
                    last = nc.tensor.transpose(pQ[oc % 2][:, mc * P:(mc + 1) * P],
                                               wffn_f[:, oc, mc * P:(mc + 1) * P], ident[:, :])
                last.then_inc(s["ffn_t"], 1)
            pe.wait_ge(s["ffn_tc"], NC)
            pe.wait_ge(s["lb4_ready"], 1)
            for ic in range(NC):
                for mc in range(NC):
                    last = mm(pC[ic][:, :], wbase_n[:, mc, ic * P:(ic + 1) * P], wffn_t[:, mc, :],
                              start=(mc == 0), stop=(mc == NC - 1))
                last.then_inc(s["m_done"], 1)
            for mc in range(NC):
                last = mm(pQ[0][:, :], lorab_4[:, mc, :, :].rearrange("p j r -> p (j r)"), wffn_t[:, mc, :],
                          start=(mc == 0), stop=(mc == NC - 1))
            last.then_inc(s["m_done"], 1)
            pe.wait_ge(s["bd_in"], 16 * TB)
            for n in range(XPARTS):
                pe.wait_ge(x_in[n], 16)
            pe.wait_ge(s["m_copied"], NC + 1)
            def mixed(n):
                if n >= 4:
                    pe.wait_ge(s["c_lo"], n - 3)
                for c in range(NC):
                    last = mm(pC[n % 4][:, c * P:(c + 1) * P], X2[:, n, c * P:(c + 1) * P], bd[:, n, :],
                              start=True, stop=True)
                last.then_inc(s["c_done"], 1)

            def first_weight_tile(r):
                if r >= 4:
                    pe.wait_ge(s["w_lo"], r - 3 + FREE)
                for c in range(NC):
                    last = nc.tensor.transpose(pW[r % 4][:, c * P:(c + 1) * P], WN[0][:, r, c * P:(c + 1) * P], ident[:, :])
                last.then_inc(s["w_t"], 1)

            for n in range(TILES - 4):
                mixed(n)
            pe.wait_ge(s["wn_in"], WEIGHTS_IN)
            for r in range(4):
                first_weight_tile(r)
            for n in range(TILES - 4, TILES):
                mixed(n)
            for r in range(4, WT):
                first_weight_tile(r)

            def weight_tile(n, i):
                pe.wait_ge(s["stage_full"], n - WT + 1)
                pe.wait_ge(s["v_lo"], i + 1 + FREE)
                for c in range(NC):
                    last = nc.tensor.transpose(pKV[:, c * P:(c + 1) * P], ST[:, c * P:(c + 1) * P], ident[:, :])
                last.then_inc(s["w_t"], 1)

            HL = ((0, 0), (0, 1), (1, 0))

            def half(h, c, lo, n):
                return (CH, CL)[h][:, c, bass.ds(lo, n)]

            def keys(i, par, blk):
                if not isinstance(i, int) or i > 0:
                    pe.wait_ge(s["x2_done"], i * 2 - 2 + FREE)
                for c in range(NC):
                    for w, h in HL:
                        last = mm(pD[:, 0:BT], WH[par][:, KT, w, c, :], half(h, c, blk * BT, BT),
                                  start=(c == 0 and w + h == 0), stop=(c == NC - 1 and w == 1))
                last.then_inc(s["k_done"], 1)

            def query(i, par, blk, g):
                pe.wait_ge(s["q_lo"], i * 2 + FREE)
                for c in range(NC):
                    for w, h in HL:
                        last = mm(pQ[g // 2][:, :].rearrange("p (b g t) -> p b g t", b=BB, g=2)[:, :, g % 2, :],
                                  WH[par][:, g, w, c, :],
                                  half(h, c, blk * BT, BT).rearrange("p (b t) -> p b t", b=BB),
                                  start=(c == 0 and w + h == 0), stop=(c == NC - 1 and w == 1))
                if g % 2:
                    last.then_inc(s["q_done"], 1)

            def transposes(i):
                pe.wait_ge(s["p_lo"], i + 1)
                pe.wait_ge(s["x2_done"], i * 2 + FREE)
                for b in range(BB):
                    last = nc.tensor.transpose(pT16[:, b * P:(b + 1) * P],
                                               PST[:, b, :, :].rearrange("p h t -> p (h t)"), ident16[:, :])
                last.then_inc(s["t_done"], 1)

            def values(i, par, blk, tiles_done):
                pe.wait_ge(s["v_lo"], i + FREE)
                if tiles_done is not None:
                    pe.wait_ge(s["w_lo"], tiles_done + FREE)
                for n in range(BTILES):
                    for c in range(NC):
                        for h, w in HL:
                            last = mm(pKV[:, n * D:(n + 1) * D], half(h, c, blk * BT + n * P, P),
                                      WH[par][:, VT, w, c, :],
                                      start=(c == 0 and w + h == 0), stop=(c == NC - 1 and h == 1))
                last.then_inc(s["v_done"], 1)

            def attend(i):
                pe.wait_ge(s["v_stacked"], (i + 1) * (16 * VDMAS) + FREE_DMA)
                pe.wait_ge(s["a_lo"], i * 2 + FREE)
                for b in range(BB):
                    if b % TB == 0:
                        pe.wait_ge(s["pt_copied"], i * 2 + (b // TB + 1))
                    last = mm(pA[b // TB][:, :].rearrange("p (g b t) -> p b g t", g=G, b=TB)[:, b % TB, :, :],
                              VST[:, b, :], PT[:, b, :].rearrange("p (g t) -> p g t", g=G),
                              start=True, stop=True)
                    if b % TB == TB - 1:
                        last.then_inc(s["a_done"], 1)

            def scores(i):
                pe.wait_ge(s["k_lo"], i + 1)
                pe.wait_ge(s["q_lo"], i * 2 + 2 + FREE)
                pe.wait_ge(s["s_read"], i + FREE)
                for b in range(BB):
                    q = [h[:, b, :, :].rearrange("p g t -> p (g t)") for h in (QH, QL)]
                    mm(pS[:, b * 2 * S:(b + 1) * 2 * S], q[0], KHL[:, b, :, :].rearrange("p h t -> p (h t)"),
                       start=True, stop=False)
                    last = mm(pS[:, b * 2 * S:b * 2 * S + S], q[1], KHL[:, b, 0, :], start=False, stop=True)
                last.then_inc(s["s_done"], 1)

            def dense(i, par, n):
                if n == 0 and not (isinstance(i, int) and i == KV * BLOCKS - 1):
                    pe.wait_ge(s["k_lo"], i + 2)
                pe.wait_ge(s["a_lo"], i * 2 + (n + 1) + FREE)
                for g in range(G):
                    for a, w in HL:
                        last = mm([pD, pT][n][:, :], (AH, AL)[a][:, g, n * P:(n + 1) * P],
                                  WH[par][:, DT:WT, w, g, :],
                                  start=(g == 0 and a + w == 0), stop=(g == G - 1 and a == 1))
                last.then_inc(s["d_done"], 1)

            def step(i, par, before, blk, prep):
                values(i, par, blk, None if prep is None else prep[0])
                if before is None:
                    pe.wait_ge(s["c_lo"], TILES)
                keys(i, par, blk)
                query(i, par, blk, 0)
                query(i, par, blk, 1)
                if before is not None:
                    transposes(i - 1)
                query(i, par, blk, 2)
                if before is not None:
                    attend(i - 1)
                query(i, par, blk, 3)
                if prep is not None:
                    weight_tile(prep[0], i)
                if before is not None:
                    dense(i - 1, before, 0)
                scores(i)
                if before is not None:
                    dense(i - 1, before, 1)

            def first(i, par, pair):
                pe.wait_ge(s["w_lo"], pair * (2 * WT) + (3 - par) * WT + FREE if par == 0
                           else pair * (2 * WT) + 2 * WT + FREE)
                step(i, par, 1 - par, 0, None)

            def begin():
                pe.wait_ge(s["c_lo"], BTILES)
                pe.wait_ge(s["w_lo"], WT + FREE)
                step(0, 0, None, 0, None)

            steps(pe, begin, first, lambda i, par, blk, prep: step(i, par, par, blk, prep))
            end = KV * BLOCKS - 1
            def scaled(n, m):
                pe.wait_ge(s["xs_ready"], n + 1)
                for c in range(NC):
                    last = nc.tensor.transpose(pQ[m][:, c * P:(c + 1) * P], XS[m][:, c * P:(c + 1) * P], ident[:, :])
                last.then_inc(s["xt_t"], 1)

            def start():
                scaled(0, 0)
                scaled(1, 1)
                transposes(end)
                low_products(0, 0)
                attend(end)
                full_products(0, 0)
                dense(end, 1, 0)
                dense(end, 1, 1)

            def low_rank_t(n, m):
                if isinstance(n, int) and n == 0:
                    pe.wait_ge(s["x2_done"], 2 * KV * BLOCKS + FREE)
                pe.wait_ge(s["low_lo"], n + 1)
                nc.tensor.transpose(pT16[:, 0:P], LOWS[m].rearrange("p h t -> p (h t)"), ident16[:, :]
                                    ).then_inc(s["low_t"], 1)

            def low_products(n, m):
                pe.wait_ge(s["m_lo"], 3)
                pe.wait_ge(s["xt_lo"], n + 1)
                if isinstance(n, int) and n == 0:
                    pe.wait_ge(s["s_read"], KV * BLOCKS + FREE)
                else:
                    pe.wait_ge(s["low_full"], n)
                for c in range(NC):
                    for h, w in HL:
                        last = mm(low_bank(n, m)[:, 0:NLAB * R], XTHL[m][:, h, c, :], LAHL[:, w, c, :],
                                  start=(c == 0 and w + h == 0), stop=(c == NC - 1 and h == 1))
                last.then_inc(s["low_done"], 1)

            def full_products(n, m):
                if isinstance(n, int) and n < 2:
                    pe.wait_ge(s["v_lo"] if n == 0 else s["a_lo"], (n + 1) * KV * BLOCKS + FREE)
                else:
                    pe.wait_ge(s["ot_ready"], n - 1 + FREE)
                for c in range(NC):
                    for h, w in HL:
                        last = mm(full_bank(n, m)[:, :], XTHL[m][:, h, c, :], MHL[:, w, c, :],
                                  start=(c == 0 and w + h == 0), stop=(c == NC - 1 and h == 1))
                last.then_inc(s["y_done"], 1)

            def low_product(n, m):
                pe.wait_ge(s["lowt_copied"], n + 1)
                pe.wait_ge(s["yb_read"], n + FREE)
                mm(pD[:, :], LOWT[m], BST, start=True, stop=True).then_inc(s["yb_done"], 1)

            tail(pe, start, scaled, low_rank_t, low_products, low_product, full_products)


_INS = ["x", "itok_B_0_15", "itok_B_0_2", "L0_cond_weights", "L0_attn_w_qkv", "L0_attn_w_dense", "L0_cond2_W",
        "L0_cond2_lora_A", "L0_cond2_lora_B_w", "L0_ffn_qweight", "L0_ffn_scale", "L0_ffn_zero_point", "L0_ffn_bias"]


def kernel(**inputs):
    import numpy as np
    import concourse.bacc as bacc
    from concourse.bass_utils import run_bass_kernel_spmd

    nc = bacc.Bacc("TRN2", target_bir_lowering=False, num_devices=1)
    arrays, args = {}, []
    for name in _INS:
        a = np.ascontiguousarray(inputs[name])
        arrays[f"in_{name}"] = a
        args.append(nc.dram_tensor(f"in_{name}", a.shape, mybir.dt.from_np(a.dtype), kind="ExternalInput").ap())
    shape = inputs["x"].shape
    args.append(nc.dram_tensor("out", shape, mybir.dt.float32, kind="ExternalOutput").ap())
    adaln_attention_ffn_kernel(nc, *args)
    r = run_bass_kernel_spmd(nc, [arrays], core_ids=[0])
    return r.results[0]["out"]
```
